# Optimizing a Trainium2 kernel written in Bass

```python
import numpy as np
import jax
import jax.numpy as jnp

def _softmax(x, axis=-1):
    return jax.nn.softmax(x, axis=axis)
def _gelu(x):
    return jax.nn.gelu(x, approximate=True)
def _silu(x):
    return jax.nn.silu(x)
def _sigmoid(x):
    return jax.nn.sigmoid(x)
def _layernorm(x, axis=-1, eps=1e-5):
    m = jnp.mean(x, axis=axis, keepdims=True)
    v = jnp.var(x, axis=axis, keepdims=True)
    return (x - m) / jnp.sqrt(v + eps)
def _scatter_add(tgt, idx, src, axis=0):
    return tgt.at[idx].add(src)
def _segment_sum(src, seg, n):
    return jax.ops.segment_sum(src, seg, n)

kernel_name = 'mk_adj_preln_d2_adj_256_894209'

def setup_inputs(seed: int = 0):
    np.random.seed(seed)
    _w = jnp.asarray
    def _rec_inputs():
        import jax
        import jax.numpy as jnp
        _gk = jax.random.key(seed)
        x = -0.0002928 + 1 * jax.random.normal(jax.random.fold_in(_gk, 1), (16, 1024, 256), jnp.float32)
        _a = jax.random.bernoulli(jax.random.fold_in(_gk, 2), 0.03125, (16, 1024, 1024))
        _a = jnp.logical_or(_a, jnp.eye(1024, dtype=bool))
        adj = _a.astype(jnp.int32)
        return x, adj
    x, adj = _rec_inputs()
    def _L0_gnn_setup():
        import jax, jax.numpy as jnp
        import numpy as np
        B, N, DIN, DOUT, H = (8, 2048, 256, 256, 8)
        HD = DOUT // H
        SCALE = HD ** (-0.5)
        key = jax.random.key(seed)
        ks = jax.random.split(key, 10)
        x = jax.random.normal(ks[0], (B, N, DIN), dtype=jnp.float32)
        adj = jax.random.randint(ks[1], (B, N, N), 0, 2, dtype=jnp.int32)
        eye = jnp.eye(N, dtype=jnp.int32)
        adj = jnp.maximum(adj, eye[None])
        s_in = (2.0 / DIN) ** 0.5
        s_out = (2.0 / DOUT) ** 0.5
        Wq = jax.random.normal(ks[2], (DOUT, DIN), dtype=jnp.float32) * s_in
        Wk = jax.random.normal(ks[3], (DOUT, DIN), dtype=jnp.float32) * s_in
        Wv = jax.random.normal(ks[4], (DOUT, DIN), dtype=jnp.float32) * s_in
        Wo = jax.random.normal(ks[5], (DOUT, DOUT), dtype=jnp.float32) * s_out
        bq = jnp.zeros((DOUT,), jnp.float32)
        bk = jnp.zeros((DOUT,), jnp.float32)
        bv = jnp.zeros((DOUT,), jnp.float32)
        bo = jnp.zeros((DOUT,), jnp.float32)
        return {'x': x, 'adj': adj, 'Wq': Wq, 'bq': bq, 'Wk': Wk, 'bk': bk, 'Wv': Wv, 'bv': bv, 'Wo': Wo, 'bo': bo}
    _L0_gnn_all = _L0_gnn_setup()
    _L0_gnn_in = {k: v for k, v in _L0_gnn_all.items() if k in ('Wq', 'bq', 'Wk', 'bk', 'Wv', 'bv', 'Wo', 'bo', )}
    del _L0_gnn_all

    def _L1_gnn_setup():
        import jax, jax.numpy as jnp
        import numpy as np
        LEAKY_SLOPE = 0.2
        NEG_INF = -9000000000000000.0

        def _edge_scores(h, a_k):
            e = jnp.einsum('bid,bjd->bij', h * a_k[:, 0], h)
            return jax.nn.leaky_relu(e, negative_slope=LEAKY_SLOPE)
        key = jax.random.key(seed)
        k1, k2, k3, k4, k5, k6 = jax.random.split(key, 6)
        B, N, D = (32, 512, 256)
        hidden = jax.random.normal(k1, (B, N, D), dtype=jnp.float32)
        adj = jax.random.randint(k2, (B, N, N), 0, 5, dtype=jnp.int32)
        a_0 = jax.random.normal(k3, (D, 1), dtype=jnp.float32)
        a_1 = jax.random.normal(k4, (D, 1), dtype=jnp.float32)
        a_2 = jax.random.normal(k5, (D, 1), dtype=jnp.float32)
        a_3 = jax.random.normal(k6, (D, 1), dtype=jnp.float32)
        return {'hidden': hidden, 'adj': adj, 'a_0': a_0, 'a_1': a_1, 'a_2': a_2, 'a_3': a_3}
    _L1_gnn_all = _L1_gnn_setup()
    _L1_gnn_in = {k: v for k, v in _L1_gnn_all.items() if k in ('a_0', 'a_1', 'a_2', 'a_3', )}
    del _L1_gnn_all

    return {
        "x": x,
        "adj": adj,
        "L0_gnn_Wq": _L0_gnn_in["Wq"],
        "L0_gnn_bq": _L0_gnn_in["bq"],
        "L0_gnn_Wk": _L0_gnn_in["Wk"],
        "L0_gnn_bk": _L0_gnn_in["bk"],
        "L0_gnn_Wv": _L0_gnn_in["Wv"],
        "L0_gnn_bv": _L0_gnn_in["bv"],
        "L0_gnn_Wo": _L0_gnn_in["Wo"],
        "L0_gnn_bo": _L0_gnn_in["bo"],
        "L1_gnn_a_0": _L1_gnn_in["a_0"],
        "L1_gnn_a_1": _L1_gnn_in["a_1"],
        "L1_gnn_a_2": _L1_gnn_in["a_2"],
        "L1_gnn_a_3": _L1_gnn_in["a_3"],
    }

def reference(x, adj, L0_gnn_Wq, L0_gnn_bq, L0_gnn_Wk, L0_gnn_bk, L0_gnn_Wv, L0_gnn_bv, L0_gnn_Wo, L0_gnn_bo, L1_gnn_a_0, L1_gnn_a_1, L1_gnn_a_2, L1_gnn_a_3):
    import jax
    import jax.numpy as jnp
    def _L0_gnn_ref(x, adj, Wq, bq, Wk, bk, Wv, bv, Wo, bo):
        import jax, jax.numpy as jnp
        import numpy as np
        B, N, DIN, DOUT, H = (8, 2048, 256, 256, 8)
        HD = DOUT // H
        SCALE = HD ** (-0.5)
        b, n, _ = x.shape

        def proj(W, bias):
            y = jnp.einsum('bnf,of->bno', x, W) + bias
            return y.reshape(b, n, H, HD).transpose(0, 2, 1, 3)
        Q, K, V = (proj(Wq, bq), proj(Wk, bk), proj(Wv, bv))
        scores = jnp.einsum('bhnd,bhmd->bhnm', Q, K) * SCALE
        mask = adj[:, None, :, :] == 0
        scores = jnp.where(mask, -jnp.inf, scores)
        attn = jax.nn.softmax(scores, axis=-1)
        attn = jnp.nan_to_num(attn, nan=0.0)
        out = jnp.einsum('bhnm,bhmd->bhnd', attn, V)
        out = out.transpose(0, 2, 1, 3).reshape(b, n, DOUT)
        return jnp.einsum('bno,po->bnp', out, Wo) + bo

    def _L1_gnn_ref(hidden, adj, a_0, a_1, a_2, a_3):
        import jax, jax.numpy as jnp
        import numpy as np
        LEAKY_SLOPE = 0.2
        NEG_INF = -9000000000000000.0

        def _edge_scores(h, a_k):
            e = jnp.einsum('bid,bjd->bij', h * a_k[:, 0], h)
            return jax.nn.leaky_relu(e, negative_slope=LEAKY_SLOPE)
        h = hidden
        e_0 = _edge_scores(h, a_0)
        e_1 = _edge_scores(h, a_1)
        e_2 = _edge_scores(h, a_2)
        e_3 = _edge_scores(h, a_3)
        scores = jnp.where(adj == 1, e_0, NEG_INF)
        scores = jnp.where(adj == 2, e_1, scores)
        scores = jnp.where(adj == 3, e_2, scores)
        scores = jnp.where(adj == 4, e_3, scores)
        alpha = jax.nn.softmax(scores, axis=-1)
        return jnp.einsum('bij,bjd->bid', alpha, h)

    h = jnp.maximum(_layernorm(x, axis=-1), 0.0)
    x = x + _L0_gnn_ref(h, adj, L0_gnn_Wq, L0_gnn_bq, L0_gnn_Wk, L0_gnn_bk, L0_gnn_Wv, L0_gnn_bv, L0_gnn_Wo, L0_gnn_bo)
    h = jnp.maximum(_layernorm(x, axis=-1), 0.0)
    x = x + _L1_gnn_ref(h, adj, L1_gnn_a_0, L1_gnn_a_1, L1_gnn_a_2, L1_gnn_a_3)
    return x


_drawn_inputs = setup_inputs


def setup_inputs(seed=0):
    import zlib

    import numpy as np

    out = dict(_drawn_inputs(seed))
    spreads = {'L0_gnn_bq': (0.0, 0.362),
     'L0_gnn_bk': (0.0, 0.8),
     'L0_gnn_bv': (0.0, 0.1),
     'L0_gnn_bo': (0.0, 0.1)}
    factors = {}
    for name, (base, spread) in spreads.items():
        noise = np.random.default_rng([zlib.crc32(name.encode()), seed]).standard_normal(out[name].shape)
        drawn = base * np.exp(spread * noise) if base else spread * noise
        out[name] = jnp.asarray(drawn.astype(out[name].dtype))
    for name, factor in factors.items():
        out[name] = (out[name] * factor).astype(out[name].dtype)
    return out
```

```python
from contextlib import ExitStack

import concourse.bass as bass
from concourse import mybir

F = mybir.dt.float32
R = mybir.dt.float32r
BF = mybir.dt.bfloat16
I32 = mybir.dt.int32
U8 = mybir.dt.uint8
ALU = mybir.AluOpType
ACT = mybir.ActivationFunctionType
AX = mybir.AxisListType.X

P = 128
B, N, D, H = 16, 1024, 256, 8
HD = D // H
NT = N // P
KT = D // P
HG = P // HD
TILES = H * NT
GROUPS = TILES // HG
QUADS = GROUPS // 4
RING = 3
SLOTS = 8
HALF = 512
HALVES = 2 * NT
SCALE = float(HD) ** -0.5
EPS = 1e-5
BIG = 1e30
SLOPE = 0.2
STK = 4 * HG * 16


def two_graph_layers(nc, x, adj, wq, bq, wk, bk, wv, bv, wo, bo, a_cols, y):
    ctx = ExitStack()
    with ctx:
        def sb(name, shape, dt):
            return ctx.enter_context(nc.sbuf_tensor(name, shape, dt))

        def sem(name):
            return ctx.enter_context(nc.semaphore(name))

        xf = sb("xf", [P, NT, D], F)
        x1 = sb("x1", [P, NT, D], F)
        adj_half = sb("adj_half", [P, 2, HALF], I32)
        bias = sb("bias", [P, NT, N], BF)
        qs = sb("qs", [P, H, N], R)
        ks = sb("ks", [P, H, N], R)
        v = sb("v", [P, NT, D], F)
        h1 = sb("h1", [P, NT, D], F)
        ot = h1[:, :, :].rearrange("p a b -> p (a b)").rearrange("p (k n) -> p k n", k=KT)
        hh = sb("hh", [P, KT, N], R)
        hl = sb("hl", [P, KT, N], R)
        hs = sb("hs", [P, 2, KT, P], F)
        ah = sb("ah", [P, 2, KT, P], R)
        al = sb("al", [P, 2, KT, P], R)
        sm = sb("sm", [P, RING, N], F)
        pt = sb("pt", [P, SLOTS, NT, P], F)
        stage = pt[:, 0:4, :, :].rearrange("p (s c) m n -> p s c (m n)", s=2).bitcast(R)
        wqh, wql = sb("wqh", [P, KT, D], R), sb("wql", [P, KT, D], R)
        wkh, wkl = sb("wkh", [P, KT, D], R), sb("wkl", [P, KT, D], R)
        wvh, wvl = sb("wvh", [P, KT, D], R), sb("wvl", [P, KT, D], R)
        wot = sb("wot", [P, KT, D], F)
        scratch = sb("scratch", [P, 2, HALF], F)
        rb = scratch[:, 0, :]
        rt = scratch[:, 1, :]
        adj_gen = scratch[:, :, :].rearrange("p a b -> p (a b)").bitcast(I32)
        eq = sb("eq", [P, N], U8)
        hg_a = sb("hg_a", [P, KT, P], F)
        bvb = sb("bvb", [P, D], F)
        bob = sb("bob", [P, D], F)
        bqc, bqs, bkc = sb("bqc", [P, KT], F), sb("bqs", [P, KT], F), sb("bkc", [P, KT], F)
        acol = sb("acol", [P, 4, KT], F)
        nacol = sb("nacol", [P, 4, KT], F)
        ident = sb("ident", [P, P], F)
        ones = sb("ones", [P, 1], F)
        mhalf = sb("mhalf", [P, NT], F)
        st = sb("st", [P, NT, 6], F)
        mv = sb("mv", [P, NT, 2], F)
        vpe = sb("vpe", [P, NT], F)
        rstd = sb("rstd", [P, NT], F)
        st1 = sb("st1", [P, NT, 6], F)
        mv1 = sb("mv1", [P, NT, 2], F)
        vpe1 = sb("vpe1", [P, NT], F)
        rstd1 = sb("rstd1", [P, NT], F)
        mn = sb("mn", [P, TILES], F)
        den = sb("den", [P, TILES], F)
        rden = sb("rden", [P, TILES], F)
        mn1 = sb("mn1", [P, NT], F)
        mnl1 = sb("mnl1", [P, NT], F)
        den1 = sb("den1", [P, NT], F)
        rden1 = sb("rden1", [P, NT], F)
        most = sb("most", [P, HALVES], F)
        most_all = sb("most_all", [P, 1], F)
        flagf = sb("flagf", [P, 1], F)
        flag = sb("flag", [1, 1], I32)

        ps = [ctx.enter_context(nc.psum_tensor(f"ps{i}", [P, N], F)) for i in range(2)]
        pT = [ctx.enter_context(nc.psum_tensor(f"pT{i}", [P, HALF], F)) for i in range(2)]
        pO = [ctx.enter_context(nc.psum_tensor(f"pO{i}", [P, HALF], F)) for i in range(2)]

        w_in = sem("w_in")
        consts = sem("consts")
        bqs_made = sem("bqs_made")
        w_tr = sem("w_tr")
        w_h = sem("w_h")
        w_l = sem("w_l")
        xf_in = sem("xf_in")
        x1_in = sem("x1_in")
        adj_in = [sem("adj_in0"), sem("adj_in1")]
        x1_bo = sem("x1_bo")
        mask_made = sem("mask_made")
        adj_most = sem("adj_most")
        f_stats, f_aggr, f_rstd, f_hn = sem("f_stats"), sem("f_aggr"), sem("f_rstd"), sem("f_hn")
        f_eps = sem("f_eps")
        f_tr, f_h, f_l = sem("f_tr"), sem("f_h"), sem("f_l")
        qk_mm, qk_h, qk_l = sem("qk_mm"), sem("qk_h"), sem("qk_l")
        stacked = [sem("stacked0"), sem("stacked1")]
        v_mm, v_made = sem("v_mm"), sem("v_made")
        flag_most, flag_f = sem("flag_most"), sem("flag_f")
        flag_mm, flag_made = sem("flag_mm"), sem("flag_made")
        s_mm, masked, exped = sem("s_mm"), sem("masked"), sem("exped")
        tr = [sem("tr0"), sem("tr1")]
        pt_made = [sem("pt_made0"), sem("pt_made1")]
        av = sem("av")
        r_rec, r_rows, r_tr, r_copied, normed = (sem(s) for s in (
            "r_rec", "r_rows", "r_tr", "r_copied", "normed"))
        o_mm, x1_made = sem("o_mm"), sem("x1_made")
        l_stats, l_aggr, l_eps, l_rstd, l_hn = (sem(s) for s in (
            "l_stats", "l_aggr", "l_eps", "l_rstd", "l_hn"))
        l_relu = sem("l_relu")
        l_tr = sem("l_tr")
        l_h, l_l = sem("l_h"), sem("l_l")
        a_sum, a_h, a_l = sem("a_sum"), sem("a_h"), sem("a_l")
        e_ready, l_masked, leaky, l_exp = (sem(s) for s in (
            "e_ready", "l_masked", "leaky", "l_exp"))
        ltr = [sem("ltr0"), sem("ltr1")]
        lpt = [sem("lpt0"), sem("lpt1")]
        pv, l_rec, y_made = sem("pv"), sem("l_rec"), sem("y_made")
        y_out = sem("y_out")
        g_adj = sem("g_adj")
        g_a = sem("g_a")
        g_e = sem("g_e")
        g_sel = sem("g_sel")
        g_chain = sem("g_chain")
        settled = sem("settled")
        GC = 3 * 3 + 3

        x_t = x.rearrange("b (t p) d -> b p t d", p=P)
        y_t = y.rearrange("b (t p) d -> b t p d", p=P)
        adj_t = adj.rearrange("b (t p) m -> b t p m", p=P)

        def settle(eng):
            eng.sem_inc(settled, 1)

        block = ctx.enter_context(nc.Block())

        @block.sync
        def _(sp):
            for i, w in enumerate((wq, wk, wv, wo)):
                sp.dma_start(x1[:, 2 * i:2 * i + 2, :],
                             w.rearrange("(t p) f -> p t f", p=P)).then_inc(w_in, 16)
            sp.dma_start(bvb[:, :], bv.rearrange("(o d) -> o d", o=1).to_broadcast([P, D])).then_inc(w_in, 16)
            sp.dma_start(bob[:, :], bo.rearrange("(o d) -> o d", o=1).to_broadcast([P, D])).then_inc(w_in, 16)
            with nc.allow_non_contiguous_dma(reason="256 values each, once"):
                sp.dma_start(bqc[:, :], bq.rearrange("(t p) -> p t", p=P)).then_inc(w_in, 16)
                sp.dma_start(bkc[:, :], bk.rearrange("(t p) -> p t", p=P)).then_inc(w_in, 16)
                for k in range(4):
                    sp.dma_start(acol[:, k, :], a_cols[k].rearrange("(t p) o -> p (t o)", p=P)).then_inc(w_in, 16)

            def load_xf(fb):
                sp.wait_ge(f_tr, KT * fb)
                sp.dma_start(xf[:, :, :], x_t[fb]).then_inc(xf_in, 16)

            def load_adj(fb, i):
                if i >= 2:
                    sp.wait_ge(mask_made, HALVES * fb + i - 1)
                    sp.wait_ge(adj_most, HALVES * fb + i - 1)
                else:
                    sp.wait_ge(mask_made, HALVES * fb)
                    sp.wait_ge(adj_most, HALVES * fb)
                c = i % 2
                sp.dma_start(adj_half[:, c, :],
                             adj_t[fb, i // 2][:, c * HALF:(c + 1) * HALF]).then_inc(adj_in[c], 16)

            def stacks(fb):
                sp.wait_ge(s_mm, TILES * fb)
                for q in range(4):
                    dst = (ks, qs)[q % 2]
                    parts = ((0, 1, 0, 1), (0, 0, 1, 1))[q % 2]
                    sp.wait_ge(qk_h, 4 * fb + q + 1)
                    sp.wait_ge(qk_l, 4 * fb + q + 1)
                    for h in range(HG):
                        for row, part in enumerate(parts):
                            sp.dma_start(dst[HD * row:HD * (row + 1), HG * (q // 2) + h, :].bitcast(F),
                                         stage[HD * h:HD * (h + 1), q % 2, part, :].bitcast(F)).then_inc(stacked[q % 2], 16)

            def general_adj(b, general, t):
                with sp.If(general > 0):
                    sp.wait_ge(g_sel, 3 * (NT * b + t))
                    sp.dma_start(adj_gen, adj_t[b, t]).then_inc(g_adj, 16)
                with sp.If(general < 1):
                    sp.sem_inc(g_adj, 16)

            def graph(b, more):
                sp.wait_ge(y_out, 16 * NT * b)
                sp.dma_start(x1[:, :, :], x_t[b]).then_inc(x1_in, 16)
                if more:
                    load_xf(b + 1)
                    stacks(b + 1)
                    load_adj(b + 1, 0)
                    load_adj(b + 1, 1)
                sp.wait_ge(flag_made, b + 1)
                settle(sp)
                general = sp.value_load(flag[0:1, 0:1], min_val=0, max_val=1)
                sp.wait_ge(normed, QUADS * (b + 1))
                settle(sp)
                general_adj(b, general, 0)
                general_adj(b, general, 1)
                for t in range(NT):
                    if more and t < NT - 1:
                        load_adj(b + 1, 2 * t + 2)
                        load_adj(b + 1, 2 * t + 3)
                    if t + 2 < NT:
                        general_adj(b, general, t + 2)
                    if t:
                        sp.wait_ge(y_made, NT * b + t)
                        sp.dma_start(y_t[b, t - 1], x1[:, t - 1, :]).then_inc(y_out, 16)
                sp.wait_ge(y_made, NT * b + NT)
                sp.dma_start(y_t[b, NT - 1], x1[:, NT - 1, :]).then_inc(y_out, 16)

            load_xf(0)
            load_adj(0, 0)
            load_adj(0, 1)
            for i in range(2, HALVES):
                load_adj(0, i)
            sp.wait_ge(w_tr, 4)
            stacks(0)
            graph(0, True)
            with sp.Fori(1, B - 1) as b:
                graph(b, True)
            graph(B - 1, False)
            sp.wait_ge(y_out, 16 * NT * B)

        @block.gpsimd
        def _(pool):
            nc.gpsimd.memset(ident[:, :], 0.0).then_inc(consts, 1)
            pool.wait_ge(consts, 1)
            nc.gpsimd.affine_select(out=ident[:, :], in_=ident[:, :], compare_op=ALU.not_equal, fill=1.0, base=0,
                                    pattern=[[-1, P]], channel_multiplier=1).then_inc(consts, 1)
            nc.gpsimd.memset(ones[:, :], 1.0).then_inc(consts, 1)
            nc.gpsimd.memset(mhalf[:, :], -0.5).then_inc(consts, 1)
            pool.wait_ge(consts, 4)

            def masks(fb, after_layer1):
                for i in range(HALVES):
                    t, c = i // 2, i % 2
                    pool.wait_ge(adj_in[c], 16 * (NT * fb + t + 1))
                    if after_layer1:
                        pool.wait_ge(l_masked, NT * fb - NT + t + 1)
                    settle(pool)
                    nc.gpsimd.tensor_scalar(bias[:, t, c * HALF:(c + 1) * HALF], adj_half[:, c, :],
                                            0.0, BIG, ALU.is_equal, ALU.mult).then_inc(mask_made, 1)

            def graph(b, more):
                pool.wait_ge(x1_in, 16 * (b + 1))
                nc.gpsimd.tensor_tensor(x1[:, :, :], x1[:, :, :],
                                        bob[:, None, :].to_broadcast([P, NT, D]), ALU.add).then_inc(x1_bo, 1)
                if more:
                    pool.wait_ge(f_eps, b + 2)
                    nc.gpsimd.tensor_tensor(rstd[:, :], vpe[:, :], mhalf[:, :], ALU.pow).then_inc(f_rstd, 1)
                pool.wait_ge(l_eps, b + 1)
                nc.gpsimd.tensor_tensor(rstd1[:, :], vpe1[:, :], mhalf[:, :], ALU.pow).then_inc(l_rstd, 1)
                if more:
                    masks(b + 1, True)

            pool.wait_ge(f_eps, 1)
            nc.gpsimd.tensor_tensor(rstd[:, :], vpe[:, :], mhalf[:, :], ALU.pow).then_inc(f_rstd, 1)
            masks(0, False)
            graph(0, True)
            with pool.Fori(1, B - 1) as b:
                graph(b, True)
            graph(B - 1, False)

        @block.scalar
        def _(act):
            for i, (dst, scale) in enumerate(((wqh, -SCALE), (wkh, 1.0), (wvh, 1.0))):
                act.wait_ge(w_tr, i + 1)
                nc.scalar.activation(dst[:, :, :].rearrange("p a b -> p (a b)"), (pO[0], pO[1], pT[0])[i][:, :],
                                     ACT.Copy, scale=scale).then_inc(w_h, 1)

            def front(fb, relu_h1):
                for k in range(KT):
                    act.wait_ge(f_tr, KT * fb + k + 1)
                    nc.scalar.activation(hh[:, k, :], ps[k][:, :], ACT.Relu).then_inc(f_h, 1)
                for q in range(4):
                    act.wait_ge(qk_mm, 4 * fb + q + 1)
                    if q < 2:
                        act.wait_ge(av, GROUPS * fb)
                    else:
                        act.wait_ge(stacked[q % 2], STK * (2 * fb + 1))
                    nc.scalar.activation(stage[:, q % 2, 0, :], ps[q % 2][:, :], ACT.Identity,
                                         bias=(bkc, bqs)[q % 2][:, q // 2:q // 2 + 1]).then_inc(qk_h, 1)
                    if q == 1:
                        relu_h1()

            def layer0(b):
                def exp(t):
                    act.wait_ge(masked, TILES * b + t + 1)
                    nc.scalar.activation(sm[:, t % RING, :], sm[:, t % RING, :], ACT.Exp, scale=-1.0,
                                         bias=mn[:, t:t + 1], accum_out=den[:, t:t + 1]).then_inc(exped, 1)

                def copy(t):
                    act.wait_ge(tr[1], TILES * b + t + 1)
                    if t >= SLOTS:
                        act.wait_ge(av, GROUPS * b + (t - SLOTS) // HG + 1)
                    else:
                        act.wait_ge(pv, NT * b)
                        act.wait_ge(stacked[0], 2 * STK * (b + 1))
                        act.wait_ge(stacked[1], 2 * STK * (b + 1))
                    nc.scalar.copy(pt[:, t % SLOTS, NT // 2:, :], pT[1][:, :].rearrange("p (m n) -> p m n", n=P)
                                   ).then_inc(pt_made[1], 1)

                def rows(quad):
                    act.wait_ge(r_tr, QUADS * b + quad + 1)
                    act.wait_ge(normed, QUADS * b + quad)
                    nc.scalar.copy(rt, pO[(quad + 1) % 2][:, :]).then_inc(r_copied, 1)

                exp(0)
                for t in range(TILES):
                    if t + 1 < TILES:
                        exp(t + 1)
                    copy(t)
                    if t and t % 16 == 0:
                        rows(t // 16 - 1)
                rows(QUADS - 1)

            def layer1(b, fronts):
                for k in range(KT):
                    act.wait_ge(l_tr, KT * b + k + 1)
                    nc.scalar.copy(hh[:, k, :], ps[k][:, :]).then_inc(l_h, 1)

                def scaled(t):
                    act.wait_ge(a_sum, NT * b + t + 1)
                    if t >= 2:
                        act.wait_ge(e_ready, NT * b + t - 1)
                    for k in range(KT):
                        last = nc.scalar.activation(ah[:, t % 2, k, :], hs[:, t % 2, k, :], ACT.Copy,
                                                    scale=nacol[:, 0, k:k + 1])
                    last.then_inc(a_h, 1)

                scaled(0)
                scaled(1)
                scaled(2)

                for t in range(NT):
                    act.wait_ge(leaky, NT * b + t + 1)
                    nc.scalar.activation(sm[:, t % RING, :], sm[:, t % RING, :], ACT.Exp, scale=-1.0,
                                         bias=mnl1[:, t:t + 1], accum_out=den1[:, t:t + 1]).then_inc(l_exp, 1)
                    if t + 3 < NT:
                        scaled(t + 3)
                    act.wait_ge(ltr[1], NT * b + t + 1)
                    slot = (SLOTS // 2 + t) % SLOTS
                    if slot < 4:
                        act.wait_ge(stacked[0], 2 * STK * fronts)
                        act.wait_ge(stacked[1], 2 * STK * fronts)
                    nc.scalar.copy(pt[:, slot, NT // 2:, :], pT[1][:, :].rearrange("p (m n) -> p m n", n=P)
                                   ).then_inc(lpt[1], 1)

            def relu_h1(b):
                for c in range(2):
                    act.wait_ge(l_hn, b + 1)
                    part = h1[:, c * NT // 2:(c + 1) * NT // 2, :]
                    nc.scalar.activation(part, part, ACT.Relu).then_inc(l_relu, 1)

            def graph(b, more):
                layer0(b)
                if more:
                    front(b + 1, lambda: relu_h1(b))
                else:
                    relu_h1(b)
                layer1(b, b + 2 if more else B)

            act.wait_ge(bqs_made, 2)
            front(0, lambda: None)
            graph(0, True)
            with act.Fori(1, B - 1) as b:
                graph(b, True)
            graph(B - 1, False)

        @block.vector
        def _(dve):
            dve.wait_ge(w_in, 16 * 12)
            nc.vector.tensor_scalar(bqs[:, :], bqc[:, :], -SCALE, None, ALU.mult).then_inc(bqs_made, 1)
            nc.vector.tensor_scalar(nacol[:, :, :], acol[:, :, :], -1.0, None, ALU.mult).then_inc(bqs_made, 1)
            dve.wait_ge(bqs_made, 2)
            for i, (dst, h, scale) in enumerate(((wql, wqh, -SCALE), (wkl, wkh, 1.0), (wvl, wvh, 1.0))):
                dve.wait_ge(w_h, i + 1)
                nc.vector.scalar_tensor_tensor(
                    out=dst[:, :, :].rearrange("p a b -> p (a b)"), in0=(pO[0], pO[1], pT[0])[i][:, :], scalar=scale,
                    in1=h[:, :, :].rearrange("p a b -> p (a b)").bitcast(F), op0=ALU.mult,
                    op1=ALU.subtract).then_inc(w_l, 1)
            dve.wait_ge(w_tr, 4)
            nc.vector.tensor_copy(wot[:, :, :].rearrange("p a b -> p (a b)"), pT[1][:, :]).then_inc(w_l, 1)

            def front_stats(fb):
                dve.wait_ge(xf_in, 16 * (fb + 1))
                for t in range(NT):
                    last = nc.vector.bn_stats(st[:, t, :], xf[:, t, :])
                last.then_inc(f_stats, 1)
                dve.wait_ge(f_stats, fb + 1)
                settle(dve)
                for t in range(NT):
                    last = nc.vector.bn_aggr(mv[:, t, :], st[:, t, :])
                last.then_inc(f_aggr, 1)
                dve.wait_ge(f_aggr, fb + 1)
                nc.vector.tensor_scalar(vpe[:, :], mv[:, :, 1], EPS, None, ALU.add).then_inc(f_eps, 1)

            def front_norm(fb):
                dve.wait_ge(f_rstd, fb + 1)
                for t in range(NT):
                    last = nc.vector.tensor_scalar(xf[:, t, :], xf[:, t, :], mv[:, t, 0:1], rstd[:, t:t + 1],
                                                   ALU.subtract, ALU.mult)
                last.then_inc(f_hn, 1)

            def front(fb, norm_h1):
                for k in range(KT):
                    dve.wait_ge(f_h, KT * fb + k + 1)
                    nc.vector.scalar_tensor_tensor(out=hl[:, k, :], in0=ps[k][:, :], scalar=0.0,
                                                   in1=hh[:, k, :].bitcast(F), op0=ALU.max,
                                                   op1=ALU.subtract).then_inc(f_l, 1)
                for q in range(4):
                    dve.wait_ge(qk_h, 4 * fb + q + 1)
                    nc.vector.scalar_tensor_tensor(
                        out=stage[:, q % 2, 1, :], in0=ps[q % 2][:, :],
                        scalar=(bkc, bqs)[q % 2][:, q // 2:q // 2 + 1], in1=stage[:, q % 2, 0, :].bitcast(F),
                        op0=ALU.add, op1=ALU.subtract).then_inc(qk_l, 1)
                    if q == 0:
                        norm_h1()
                    if q % 2:
                        for t in range(NT // 2 * (q // 2), NT // 2 * (q // 2 + 1)):
                            dve.wait_ge(v_mm, NT * fb + t + 1)
                            nc.vector.tensor_tensor(v[:, t, :], pO[t % 2][:, 0:D], bvb[:, :],
                                                    ALU.add).then_inc(v_made, 1)

            def most_half(fb, i):
                dve.wait_ge(adj_in[i % 2], 16 * (NT * fb + i // 2 + 1))
                nc.vector.tensor_reduce(most[:, i:i + 1], adj_half[:, i % 2, :], AX, ALU.max,
                                        apply_absolute_value=True).then_inc(adj_most, 1)

            def flag_rows(fb):
                dve.wait_ge(adj_most, HALVES * (fb + 1))
                nc.vector.tensor_reduce(most_all[:, :], most[:, :], AX, ALU.max).then_inc(flag_most, 1)
                dve.wait_ge(flag_most, fb + 1)
                nc.vector.tensor_scalar(flagf[:, :], most_all[:, :], 1.5, None, ALU.is_gt).then_inc(flag_f, 1)

            def layer0(b, more):
                dve.wait_ge(flag_mm, b + 1)
                nc.vector.tensor_scalar(flag[:, :], pO[1][0:1, 0:1], 1.0, None, ALU.min).then_inc(flag_made, 1)

                def mask(t):
                    node = t // HG % NT
                    dve.wait_ge(s_mm, TILES * b + t + 1)
                    dve.wait_ge(mask_made, HALVES * b + 2 * node + 2)
                    if t >= RING:
                        dve.wait_ge(tr[1], TILES * b + t - RING + 1)
                    else:
                        dve.wait_ge(ltr[1], NT * b)
                    settle(dve)
                    nc.vector.tensor_tensor_reduce(
                        out=sm[:, t % RING, :], in0=ps[t % 2][:, :], in1=bias[:, node, :], scale=1.0, scalar=3e38,
                        op0=ALU.add, op1=ALU.min, accum_out=mn[:, t:t + 1]).then_inc(masked, 1)

                def copy(t):
                    dve.wait_ge(tr[0], TILES * b + t + 1)
                    if t >= SLOTS:
                        dve.wait_ge(av, GROUPS * b + (t - SLOTS) // HG + 1)
                    else:
                        dve.wait_ge(pv, NT * b)
                        dve.wait_ge(stacked[0], 2 * STK * (b + 1))
                        dve.wait_ge(stacked[1], 2 * STK * (b + 1))
                    nc.vector.tensor_copy(pt[:, t % SLOTS, 0:NT // 2, :],
                                          pT[0][:, :].rearrange("p (m n) -> p m n", n=P)).then_inc(pt_made[0], 1)

                def rows(quad):
                    cols = slice(16 * quad, 16 * quad + 16)
                    dve.wait_ge(exped, TILES * b + 16 * quad + 16)
                    nc.vector.reciprocal(rden[:, cols], den[:, cols]).then_inc(r_rec, 1)
                    dve.wait_ge(r_rec, QUADS * b + quad + 1)
                    dve.wait_ge(r_tr, QUADS * b + quad)
                    nc.vector.scalar_tensor_tensor(
                        out=rb.rearrange("p (c w) -> p c w", w=HD),
                        in0=mn[:, cols].rearrange("p (c o) -> p c o", o=1).to_broadcast([P, 16, HD]), scalar=BIG / 10,
                        in1=rden[:, cols].rearrange("p (c o) -> p c o", o=1).to_broadcast([P, 16, HD]),
                        op0=ALU.is_lt, op1=ALU.mult).then_inc(r_rows, 1)

                def norm(quad):
                    dve.wait_ge(r_copied, QUADS * b + quad + 1)
                    dve.wait_ge(av, GROUPS * b + 4 * quad + 4)
                    if quad == 0:
                        dve.wait_ge(pv, NT * b)
                    nc.vector.tensor_tensor(ot[:, quad // 2, HALF * (quad % 2):HALF * (quad % 2 + 1)],
                                            pO[quad % 2][:, :], rt, ALU.mult).then_inc(normed, 1)

                mask(0)
                mask(1)
                for t in range(TILES):
                    if t + 2 < TILES:
                        mask(t + 2)
                    copy(t)
                    if t % 16 == 15:
                        rows(t // 16)
                    if t > 16 and t % 16 == 4:
                        norm(t // 16 - 1)
                    if more and t == 42:
                        front_stats(b + 1)
                    if more and t == 46:
                        front_norm(b + 1)
                norm(QUADS - 1)

            def output(b):
                dve.wait_ge(x1_bo, b + 1)
                for t in range(NT):
                    dve.wait_ge(o_mm, NT * b + t + 1)
                    nc.vector.tensor_tensor(x1[:, t, :], pT[t % 2][:, 0:D], x1[:, t, :], ALU.add).then_inc(x1_made, 1)
                    if t:
                        dve.wait_ge(x1_made, NT * b + t)
                        nc.vector.bn_stats(st1[:, t - 1, :], x1[:, t - 1, :])
                dve.wait_ge(x1_made, NT * b + NT)
                nc.vector.bn_stats(st1[:, NT - 1, :], x1[:, NT - 1, :]).then_inc(l_stats, 1)
                dve.wait_ge(l_stats, b + 1)
                settle(dve)
                for t in range(NT):
                    last = nc.vector.bn_aggr(mv1[:, t, :], st1[:, t, :])
                last.then_inc(l_aggr, 1)
                dve.wait_ge(l_aggr, b + 1)
                nc.vector.tensor_scalar(vpe1[:, :], mv1[:, :, 1], EPS, None, ALU.add).then_inc(l_eps, 1)

            def norm_h1(b):
                dve.wait_ge(l_rstd, b + 1)
                dve.wait_ge(o_mm, NT * (b + 1))
                for t in range(NT):
                    last = nc.vector.tensor_scalar(h1[:, t, :], x1[:, t, :], mv1[:, t, 0:1], rstd1[:, t:t + 1],
                                                   ALU.subtract, ALU.mult)
                last.then_inc(l_hn, 1)

            def layer1(b, fronts, more, general):
                for k in range(KT):
                    dve.wait_ge(l_h, KT * b + k + 1)
                    nc.vector.tensor_tensor(hl[:, k, :], ps[k][:, :], hh[:, k, :].bitcast(F),
                                            ALU.subtract).then_inc(l_l, 1)
                dve.wait_ge(l_l, KT * (b + 1))

                def whole(t):
                    if t >= 2:
                        dve.wait_ge(a_h, NT * b + t - 1)
                        dve.wait_ge(a_l, NT * b + t - 1)
                    cols = slice(t * P, (t + 1) * P)
                    nc.vector.tensor_tensor(hs[:, t % 2, :, :], hh[:, :, cols].bitcast(F),
                                            hl[:, :, cols].bitcast(F), ALU.add).then_inc(a_sum, 1)

                def scaled(t):
                    dve.wait_ge(a_h, NT * b + t + 1)
                    if t >= 2:
                        dve.wait_ge(e_ready, NT * b + t - 1)
                    for k in range(KT):
                        last = nc.vector.scalar_tensor_tensor(
                            out=al[:, t % 2, k, :], in0=hs[:, t % 2, k, :], scalar=nacol[:, 0, k:k + 1],
                            in1=ah[:, t % 2, k, :].bitcast(F), op0=ALU.mult, op1=ALU.subtract)
                    last.then_inc(a_l, 1)

                def select(t):
                    with dve.If(general > 0):
                        n = [GC * (NT * b + t)]

                        def link(ins):
                            n[0] = n[0] + 1
                            ins.then_inc(g_chain, 1)
                            dve.wait_ge(g_chain, n[0])
                            settle(dve)

                        dve.wait_ge(g_adj, 16 * (NT * b + t + 1))
                        dve.wait_ge(a_sum, NT * b + t + 1)
                        dve.wait_ge(g_e, 4 * (NT * b + t) + 1)
                        for k in range(1, 4):
                            for kt in range(KT):
                                last = nc.vector.tensor_scalar(hg_a[:, kt, :], hs[:, t % 2, kt, :],
                                                               nacol[:, k, kt:kt + 1], None, ALU.mult)
                                if kt < KT - 1:
                                    link(last)
                            last.then_inc(g_a, 1)
                            link(nc.vector.tensor_scalar(eq[:, :], adj_gen, float(k + 1), None, ALU.is_equal))
                            dve.wait_ge(g_e, 4 * (NT * b + t) + k + 1)
                            settle(dve)
                            link(nc.vector.copy_predicated(ps[t % 2][:, 0:HALF], eq[:, 0:HALF], pO[0][:, :]))
                            if k < 3:
                                nc.vector.copy_predicated(ps[t % 2][:, HALF:N], eq[:, HALF:N],
                                                          pO[1][:, :]).then_inc(g_sel, 1)
                                dve.wait_ge(g_sel, 3 * (NT * b + t) + k)
                            else:
                                link(nc.vector.copy_predicated(ps[t % 2][:, HALF:N], eq[:, HALF:N], pO[1][:, :]))
                        link(nc.vector.tensor_scalar(eq[:, :], adj_gen, 0.5, None, ALU.is_lt))
                        link(nc.vector.tensor_scalar(bias[:, t, :], adj_gen, 4.5, BIG, ALU.is_gt, ALU.mult))
                        nc.vector.scalar_tensor_tensor(out=bias[:, t, :], in0=eq[:, :], scalar=BIG,
                                                       in1=bias[:, t, :], op0=ALU.mult,
                                                       op1=ALU.max).then_inc(g_sel, 1)
                        dve.wait_ge(g_sel, 3 * (NT * b + t) + 3)
                        settle(dve)
                    with dve.If(general < 1):
                        dve.sem_inc(g_chain, GC)
                        dve.sem_inc(g_a, 3)
                        dve.sem_inc(g_sel, 3)

                def mask(t):
                    dve.wait_ge(e_ready, NT * b + t + 1)
                    if t >= RING:
                        dve.wait_ge(ltr[1], NT * b + t - RING + 1)
                    else:
                        dve.wait_ge(tr[1], TILES * (b + 1))
                    settle(dve)
                    nc.vector.tensor_tensor_reduce(
                        out=sm[:, t % RING, :], in0=ps[t % 2][:, :], in1=bias[:, t, :], scale=1.0, scalar=3e38,
                        op0=ALU.add, op1=ALU.min, accum_out=mn1[:, t:t + 1]).then_inc(l_masked, 1)
                    dve.wait_ge(l_masked, NT * b + t + 1)
                    nc.vector.scalar_tensor_tensor(out=mnl1[:, t:t + 1], in0=mn1[:, t:t + 1], scalar=SLOPE,
                                                   in1=mn1[:, t:t + 1], op0=ALU.mult, op1=ALU.min)
                    nc.vector.scalar_tensor_tensor(out=sm[:, t % RING, :], in0=sm[:, t % RING, :], scalar=SLOPE,
                                                   in1=sm[:, t % RING, :], op0=ALU.mult,
                                                   op1=ALU.min).then_inc(leaky, 1)

                def most_tile(t):
                    most_half(b + 1, 2 * t)
                    most_half(b + 1, 2 * t + 1)

                def copy(t):
                    dve.wait_ge(ltr[0], NT * b + t + 1)
                    slot = (SLOTS // 2 + t) % SLOTS
                    if slot < 4:
                        dve.wait_ge(stacked[0], 2 * STK * fronts)
                        dve.wait_ge(stacked[1], 2 * STK * fronts)
                    nc.vector.tensor_copy(pt[:, slot, 0:NT // 2, :],
                                          pT[0][:, :].rearrange("p (m n) -> p m n", n=P)).then_inc(lpt[0], 1)

                def result(t):
                    dve.wait_ge(l_exp, NT * b + t + 1)
                    nc.vector.reciprocal(rden1[:, t:t + 1], den1[:, t:t + 1]).then_inc(l_rec, 1)
                    dve.wait_ge(l_rec, NT * b + t + 1)
                    dve.wait_ge(pv, NT * b + t + 1)
                    nc.vector.scalar_tensor_tensor(out=x1[:, t, :], in0=pO[t % 2][:, 0:D], scalar=rden1[:, t:t + 1],
                                                   in1=x1[:, t, :], op0=ALU.mult, op1=ALU.add).then_inc(y_made, 1)

                whole(0)
                whole(1)
                scaled(0)
                scaled(1)
                select(0)
                mask(0)
                if more:
                    most_tile(0)
                whole(2)
                scaled(2)
                select(1)
                for t in range(NT):
                    if t + 1 < NT:
                        mask(t + 1)
                    if t + 3 < NT:
                        whole(t + 3)
                        if more:
                            most_tile(t + 1)
                        scaled(t + 3)
                    elif more and t + 1 < NT:
                        most_tile(t + 1)
                    if t + 2 < NT:
                        select(t + 2)
                    copy(t)
                    if t:
                        result(t - 1)
                result(NT - 1)
                if more:
                    flag_rows(b + 1)

            def graph(b, more):
                layer0(b, more)
                output(b)
                if more:
                    front(b + 1, lambda: norm_h1(b))
                else:
                    norm_h1(b)
                dve.wait_ge(flag_made, b + 1)
                settle(dve)
                general = dve.value_load(flag[0:1, 0:1], min_val=0, max_val=1)
                layer1(b, b + 2 if more else B, more, general)

            front_stats(0)
            front_norm(0)
            for i in range(HALVES):
                most_half(0, i)
            flag_rows(0)
            front(0, lambda: None)
            graph(0, True)
            with dve.Fori(1, B - 1) as b:
                graph(b, True)
            graph(B - 1, False)

        @block.tensor
        def _(pe):
            pe.wait_ge(w_in, 16 * 12)
            pe.wait_ge(consts, 4)
            for i, out in enumerate((pO[0], pO[1], pT[0], pT[1])):
                for ft in range(KT):
                    for o in range(KT):
                        last = nc.tensor.transpose(out[:, ft * D + o * P:ft * D + (o + 1) * P],
                                                   x1[:, 2 * i + o, ft * P:(ft + 1) * P], ident[:, :])
                last.then_inc(w_tr, 1)

            def split_product(out, lhs, rhs, start, stop):
                terms = ((lhs[0], rhs[0]), (lhs[0], rhs[1]), (lhs[1], rhs[0]))
                for i, (a, c) in enumerate(terms):
                    last = nc.tensor.matmul(out, a, c, start=start and i == 0, stop=stop and i == len(terms) - 1)
                return last

            def transpose_h(src, b, done):
                for k in range(KT):
                    for t in range(NT):
                        last = nc.tensor.transpose(ps[k][:, t * P:(t + 1) * P], src[:, t, k * P:(k + 1) * P],
                                                   ident[:, :])
                    last.then_inc(done, 1)

            def front(fb):
                pe.wait_ge(f_hn, fb + 1)
                pe.wait_ge(masked, TILES * fb)
                transpose_h(xf, fb, f_tr)

                def qk(q):
                    wh, wl = ((wkh, wkl), (wqh, wql))[q % 2]
                    pe.wait_ge(f_l, KT * (fb + 1))
                    if q >= 2:
                        pe.wait_ge(qk_l, 4 * fb + q - 1)
                    o = slice((q // 2) * P, (q // 2 + 1) * P)
                    for c in range(2):
                        n = slice(c * HALF, (c + 1) * HALF)
                        for k in range(KT):
                            last = split_product(ps[q % 2][:, n], (wh[:, k, o], wl[:, k, o]),
                                                 (hh[:, k, n], hl[:, k, n]), k == 0, k == KT - 1)
                    last.then_inc(qk_mm, 1)

                def value(t):
                    if t >= 2:
                        pe.wait_ge(v_made, NT * fb + t - 1)
                    else:
                        pe.wait_ge(normed, QUADS * fb)
                        pe.wait_ge(r_copied, QUADS * fb)
                    n = slice(t * P, (t + 1) * P)
                    for k in range(KT):
                        last = split_product(pO[t % 2][:, 0:D], (hh[:, k, n], hl[:, k, n]),
                                             (wvh[:, k, :], wvl[:, k, :]), k == 0, k == KT - 1)
                    last.then_inc(v_mm, 1)

                qk(0)
                qk(1)
                for t in range(NT // 2):
                    value(t)
                qk(2)
                qk(3)
                for t in range(NT // 2, NT):
                    value(t)

            def layer0(b):
                pe.wait_ge(y_made, NT * b)
                pe.wait_ge(v_made, NT * (b + 1))
                pe.wait_ge(flag_f, b + 1)
                nc.tensor.matmul(pO[1][0:1, 0:1], flagf[:, :], ones[:, :], start=True, stop=True).then_inc(flag_mm, 1)

                def scores(t):
                    hg, node, h = t // (HG * NT), t // HG % NT, t % HG
                    head = HG * hg + h
                    if t % (HG * NT) == 0:
                        pe.wait_ge(stacked[0], STK * (2 * b + hg + 1))
                        pe.wait_ge(stacked[1], STK * (2 * b + hg + 1))
                    if t >= 2:
                        pe.wait_ge(masked, TILES * b + t - 1)
                    else:
                        pe.wait_ge(l_masked, NT * b)
                        pe.wait_ge(qk_l, 4 * (b + 1))
                    for c in range(2):
                        last = nc.tensor.matmul(ps[t % 2][:, c * HALF:(c + 1) * HALF],
                                                qs[:, head, node * P:(node + 1) * P],
                                                ks[:, head, c * HALF:(c + 1) * HALF], start=True, stop=True)
                    last.then_inc(s_mm, 1)

                def transposes(t):
                    pe.wait_ge(exped, TILES * b + t + 1)
                    for c in range(2):
                        pe.wait_ge(pt_made[c], TILES * b + t)
                        if t == 0:
                            pe.wait_ge(lpt[c], NT * b)
                        for j in range(4):
                            m = 4 * c + j
                            last = nc.tensor.transpose(pT[c][:, j * P:(j + 1) * P],
                                                       sm[:, t % RING, m * P:(m + 1) * P], ident[:, :])
                        last.then_inc(tr[c], 1)

                def values(g, part):
                    hg, quad = g // NT, g // 4
                    if part == 0:
                        pe.wait_ge(pt_made[0], TILES * b + HG * (g + 1))
                        pe.wait_ge(pt_made[1], TILES * b + HG * (g + 1))
                    if g % 4 == 0 and quad and part == 0:
                        pe.wait_ge(r_copied, QUADS * b + quad)
                        pe.wait_ge(normed, QUADS * b + quad - 1)
                    n = slice(g % 4 * P, (g % 4 + 1) * P)
                    for m in range(NT // 4 * part, NT // 4 * (part + 1)):
                        for h in range(HG):
                            o = (HG * hg + h) * HD
                            last = nc.tensor.matmul(pO[quad % 2][HD * h:HD * (h + 1), n], v[:, m, o:o + HD],
                                                    pt[:, (HG * g + h) % SLOTS, m, :], start=(m == 0),
                                                    stop=(m == NT - 1))
                    if part == 3:
                        last.then_inc(av, 1)

                def rows(quad):
                    pe.wait_ge(r_rows, QUADS * b + quad + 1)
                    pe.wait_ge(normed, QUADS * b + quad)
                    pe.wait_ge(flag_made, b + 1)
                    for j in range(4):
                        last = nc.tensor.transpose(pO[(quad + 1) % 2][:, j * P:(j + 1) * P], rb[:, j * P:(j + 1) * P],
                                                   ident[:, :])
                    last.then_inc(r_tr, 1)

                scores(0)
                scores(1)
                for t in range(TILES):
                    if t + 2 < TILES:
                        scores(t + 2)
                    transposes(t)
                    if t >= HG:
                        values(t // HG - 1, t % HG)
                    if t and t % 16 == 0:
                        rows(t // 16 - 1)
                for part in range(4):
                    values(GROUPS - 1, part)
                rows(QUADS - 1)

            def output(b):
                pe.wait_ge(normed, QUADS * (b + 1))
                for t in range(NT):
                    if t < 2:
                        pe.wait_ge(pt_made[t], TILES * (b + 1))
                    else:
                        pe.wait_ge(x1_made, NT * b + t - 1)
                    for k in range(KT):
                        last = nc.tensor.matmul(pT[t % 2][:, 0:D], ot[:, k, t * P:(t + 1) * P], wot[:, k, :],
                                                start=(k == 0), stop=(k == KT - 1))
                    last.then_inc(o_mm, 1)

            def layer1(b, fronts, general):
                pe.wait_ge(l_relu, 2 * (b + 1))
                pe.wait_ge(masked, TILES * (b + 1))
                pe.wait_ge(qk_l, 4 * fronts)
                transpose_h(h1, b, l_tr)

                def edges(t):
                    pe.wait_ge(a_l, NT * b + t + 1)
                    if t >= 2:
                        pe.wait_ge(l_masked, NT * b + t - 1)

                    def first():
                        for c in range(2):
                            n = slice(c * HALF, (c + 1) * HALF)
                            for k in range(KT):
                                last = split_product(ps[t % 2][:, n], (ah[:, t % 2, k, :], al[:, t % 2, k, :]),
                                                     (hh[:, k, n], hl[:, k, n]), k == 0, k == KT - 1)
                        return last

                    with pe.If(general > 0):
                        first().then_inc(g_e, 1)
                        pe.wait_ge(v_made, NT * fronts)
                        pe.wait_ge(y_made, NT * b + max(t - 3, 0))
                        for kind in range(1, 4):
                            pe.wait_ge(g_a, 3 * (NT * b + t) + kind)
                            if kind > 1:
                                pe.wait_ge(g_sel, 3 * (NT * b + t) + kind - 1)
                            for c in range(2):
                                n = slice(c * HALF, (c + 1) * HALF)
                                for k in range(KT):
                                    for part in (hh, hl):
                                        last = nc.tensor.matmul(pO[c][:, :], hg_a[:, k, :],
                                                                part[:, k, n].bitcast(F),
                                                                start=(k == 0 and part is hh),
                                                                stop=(k == KT - 1 and part is hl))
                            last.then_inc(g_e, 1)
                        pe.wait_ge(g_sel, 3 * (NT * b + t) + 3)
                        pe.sem_inc(e_ready, 1)
                    with pe.If(general < 1):
                        first().then_inc(e_ready, 1)
                        pe.sem_inc(g_e, 4)

                def transposes(t):
                    pe.wait_ge(l_exp, NT * b + t + 1)
                    for c in range(2):
                        pe.wait_ge(lpt[c], NT * b + t)
                        if t == 0:
                            pe.wait_ge(x1_made, NT * (b + 1))
                        for j in range(4):
                            m = 4 * c + j
                            last = nc.tensor.transpose(pT[c][:, j * P:(j + 1) * P],
                                                       sm[:, t % RING, m * P:(m + 1) * P], ident[:, :])
                        last.then_inc(ltr[c], 1)

                def values(t):
                    pe.wait_ge(lpt[0], NT * b + t + 1)
                    pe.wait_ge(lpt[1], NT * b + t + 1)
                    if t >= 2:
                        pe.wait_ge(y_made, NT * b + t - 1)
                    else:
                        pe.wait_ge(v_made, NT * fronts)
                    slot = (SLOTS // 2 + t) % SLOTS
                    for m in range(NT):
                        last = nc.tensor.matmul(pO[t % 2][:, 0:D], pt[:, slot, m, :], h1[:, m, :],
                                                start=(m == 0), stop=(m == NT - 1))
                    last.then_inc(pv, 1)

                edges(0)
                edges(1)
                for t in range(NT):
                    if t + 2 < NT:
                        edges(t + 2)
                    transposes(t)
                    if t:
                        values(t - 1)
                values(NT - 1)

            def graph(b, more):
                layer0(b)
                output(b)
                if more:
                    front(b + 1)
                pe.wait_ge(flag_made, b + 1)
                settle(pe)
                general = pe.value_load(flag[0:1, 0:1], min_val=0, max_val=1)
                layer1(b, b + 2 if more else B, general)

            pe.wait_ge(w_l, 4)
            front(0)
            graph(0, True)
            with pe.Fori(1, B - 1) as b:
                graph(b, True)
            graph(B - 1, False)


_INS = ["x", "adj", "L0_gnn_Wq", "L0_gnn_bq", "L0_gnn_Wk", "L0_gnn_bk", "L0_gnn_Wv", "L0_gnn_bv",
        "L0_gnn_Wo", "L0_gnn_bo", "L1_gnn_a_0", "L1_gnn_a_1", "L1_gnn_a_2", "L1_gnn_a_3"]


def kernel(**inputs):
    import numpy as _np
    import concourse.bacc as _bacc
    from concourse import mybir as _mybir
    from concourse.bass_utils import run_bass_kernel_spmd as _run

    nc = _bacc.Bacc("TRN2", target_bir_lowering=False, num_devices=1)
    arrays, args = {}, []
    for name in _INS:
        a = _np.ascontiguousarray(inputs[name])
        arrays[f"in_{name}_dram"] = a
        args.append(nc.dram_tensor(f"in_{name}_dram", a.shape, _mybir.dt.from_np(a.dtype), kind="ExternalInput").ap())
    out = nc.dram_tensor("out_0_dram", (B, N, D), F, kind="ExternalOutput").ap()
    two_graph_layers(nc, *args[:10], args[10:14], out)
    r = _run(nc, [arrays], core_ids=[0])
    return r.results[0]["out_0_dram"]
```

```python
from contextlib import ExitStack

import concourse.bass as bass
from concourse import mybir

F = mybir.dt.float32
R = mybir.dt.float32r
BF = mybir.dt.bfloat16
I32 = mybir.dt.int32
U8 = mybir.dt.uint8
ALU = mybir.AluOpType
ACT = mybir.ActivationFunctionType
AX = mybir.AxisListType.X

P = 128
B, N, D, H = 16, 1024, 256, 8
HD = D // H
NT = N // P
KT = D // P
HG = P // HD
TILES = H * NT
GROUPS = TILES // HG
QUADS = GROUPS // 4
RING = 3
SLOTS = 8
HALF = 512
HALVES = 2 * NT
SCALE = float(HD) ** -0.5
EPS = 1e-5
BIG = 1e30
SLOPE = 0.2
ROWS = 3 * HD
STK = 3 * HG * 16


def two_graph_layers(nc, x, adj, wq, bq, wk, bk, wv, bv, wo, bo, a_cols, y):
    ctx = ExitStack()
    with ctx:
        def sb(name, shape, dt):
            return ctx.enter_context(nc.sbuf_tensor(name, shape, dt))

        def sem(name):
            return ctx.enter_context(nc.semaphore(name))

        xf = sb("xf", [P, NT, D], F)
        x1 = sb("x1", [P, NT, D], F)
        adj_half = sb("adj_half", [P, 2, HALF], I32)
        bias = sb("bias", [P, NT, N], BF)
        qs = sb("qs", [ROWS, H, N], R)
        ks = sb("ks", [ROWS, H, N], R)
        v = sb("v", [P, NT, D], F)
        h1 = sb("h1", [P, NT, D], F)
        ot = h1[:, :, :].rearrange("p a b -> p (a b)").rearrange("p (k n) -> p k n", k=KT)
        hh = sb("hh", [P, KT, N], R)
        hl = sb("hl", [P, KT, N], R)
        hs = sb("hs", [P, 2, KT, P], F)
        ah = sb("ah", [P, 2, KT, P], R)
        al = sb("al", [P, 2, KT, P], R)
        sm = sb("sm", [P, RING, N], F)
        pt = sb("pt", [P, SLOTS, NT, P], F)
        stage = pt[:, :, :, :].rearrange("p (q c) m n -> p q c (m n)", q=4).bitcast(R)
        wqh, wql = sb("wqh", [P, KT, D], R), sb("wql", [P, KT, D], R)
        wkh, wkl = sb("wkh", [P, KT, D], R), sb("wkl", [P, KT, D], R)
        wvh, wvl = sb("wvh", [P, KT, D], R), sb("wvl", [P, KT, D], R)
        wot = sb("wot", [P, KT, D], F)
        scratch = sb("scratch", [P, 2, HALF], F)
        rb = scratch[:, 0, :]
        rt = scratch[:, 1, :]
        adj_gen = scratch[:, :, :].rearrange("p a b -> p (a b)").bitcast(I32)
        eq = sb("eq", [P, N], U8)
        hg_a = sb("hg_a", [P, KT, P], F)
        bvb = sb("bvb", [P, D], F)
        bob = sb("bob", [P, D], F)
        bqc, bqs, bkc = sb("bqc", [P, KT], F), sb("bqs", [P, KT], F), sb("bkc", [P, KT], F)
        acol = sb("acol", [P, 4, KT], F)
        nacol = sb("nacol", [P, 4, KT], F)
        ident = sb("ident", [P, P], F)
        ones = sb("ones", [P, 1], F)
        mhalf = sb("mhalf", [P, NT], F)
        st = sb("st", [P, NT, 6], F)
        mv = sb("mv", [P, NT, 2], F)
        vpe = sb("vpe", [P, NT], F)
        rstd = sb("rstd", [P, NT], F)
        nmean = sb("nmean", [P, NT], F)
        st1 = sb("st1", [P, NT, 6], F)
        mv1 = sb("mv1", [P, NT, 2], F)
        vpe1 = sb("vpe1", [P, NT], F)
        rstd1 = sb("rstd1", [P, NT], F)
        mn = sb("mn", [P, TILES], F)
        den = sb("den", [P, TILES], F)
        rden = sb("rden", [P, TILES], F)
        mn1 = sb("mn1", [P, NT], F)
        mnl1 = sb("mnl1", [P, NT], F)
        den1 = sb("den1", [P, NT], F)
        rden1 = sb("rden1", [P, NT], F)
        most = sb("most", [P, HALVES], F)
        most_all = sb("most_all", [P, 1], F)
        flagf = sb("flagf", [P, 1], F)
        flag = sb("flag", [1, 1], I32)

        ps = [ctx.enter_context(nc.psum_tensor(f"ps{i}", [P, N], F)) for i in range(2)]
        pT = [ctx.enter_context(nc.psum_tensor(f"pT{i}", [P, HALF], F)) for i in range(2)]
        pO = [ctx.enter_context(nc.psum_tensor(f"pO{i}", [P, HALF], F)) for i in range(2)]

        w_in = sem("w_in")
        consts = sem("consts")
        bqs_made = sem("bqs_made")
        w_tr = sem("w_tr")
        w_h = sem("w_h")
        w_l = sem("w_l")
        xf_in = sem("xf_in")
        x1_in = sem("x1_in")
        adj_in = [sem("adj_in0"), sem("adj_in1")]
        x1_bo = sem("x1_bo")
        mask_made = sem("mask_made")
        adj_most = sem("adj_most")
        f_stats, f_aggr, f_rstd, f_hn = sem("f_stats"), sem("f_aggr"), sem("f_rstd"), sem("f_hn")
        f_eps = sem("f_eps")
        f_tr, f_h, f_l = sem("f_tr"), sem("f_h"), sem("f_l")
        qk_mm, qk_h, qk_l = sem("qk_mm"), sem("qk_h"), sem("qk_l")
        stacked = [sem(f"stacked{q}") for q in range(4)]
        v_mm, v_made = sem("v_mm"), sem("v_made")
        flag_most, flag_f = sem("flag_most"), sem("flag_f")
        flag_mm, flag_made = sem("flag_mm"), sem("flag_made")
        s_mm, masked, exped = sem("s_mm"), sem("masked"), sem("exped")
        tr = [sem("tr0"), sem("tr1")]
        pt_made = [sem("pt_made0"), sem("pt_made1")]
        av = sem("av")
        r_rec, r_rows, r_tr, r_copied, normed = (sem(s) for s in (
            "r_rec", "r_rows", "r_tr", "r_copied", "normed"))
        o_mm, x1_made = sem("o_mm"), sem("x1_made")
        l_stats, l_aggr, l_eps, l_rstd, l_hn = (sem(s) for s in (
            "l_stats", "l_aggr", "l_eps", "l_rstd", "l_hn"))
        l_relu = sem("l_relu")
        l_tr = sem("l_tr")
        l_h, l_l = sem("l_h"), sem("l_l")
        a_sum, a_h, a_l = sem("a_sum"), sem("a_h"), sem("a_l")
        e_ready, l_masked, leaky, l_exp = (sem(s) for s in (
            "e_ready", "l_masked", "leaky", "l_exp"))
        ltr = [sem("ltr0"), sem("ltr1")]
        lpt = [sem("lpt0"), sem("lpt1")]
        pv, l_rec, y_made = sem("pv"), sem("l_rec"), sem("y_made")
        y_out = sem("y_out")
        g_adj = sem("g_adj")
        g_a = sem("g_a")
        g_e = sem("g_e")
        g_sel = sem("g_sel")
        g_chain = sem("g_chain")
        settled = sem("settled")
        GC = 3 * 3 + 3

        x_t = x.rearrange("b (t p) d -> b p t d", p=P)
        y_t = y.rearrange("b (t p) d -> b t p d", p=P)
        adj_t = adj.rearrange("b (t p) m -> b t p m", p=P)

        def settle(eng):
            eng.sem_inc(settled, 1)

        block = ctx.enter_context(nc.Block())

        @block.sync
        def _(sp):
            for i, w in enumerate((wq, wk, wv, wo)):
                sp.dma_start(x1[:, 2 * i:2 * i + 2, :],
                             w.rearrange("(t p) f -> p t f", p=P)).then_inc(w_in, 16)
            sp.dma_start(bvb[:, :], bv.rearrange("(o d) -> o d", o=1).to_broadcast([P, D])).then_inc(w_in, 16)
            sp.dma_start(bob[:, :], bo.rearrange("(o d) -> o d", o=1).to_broadcast([P, D])).then_inc(w_in, 16)
            with nc.allow_non_contiguous_dma(reason="256 values each, once"):
                sp.dma_start(bqc[:, :], bq.rearrange("(t p) -> p t", p=P)).then_inc(w_in, 16)
                sp.dma_start(bkc[:, :], bk.rearrange("(t p) -> p t", p=P)).then_inc(w_in, 16)
                for k in range(4):
                    sp.dma_start(acol[:, k, :], a_cols[k].rearrange("(t p) o -> p (t o)", p=P)).then_inc(w_in, 16)

            def load_xf(fb):
                sp.wait_ge(f_tr, KT * fb)
                sp.dma_start(xf[:, :, :], x_t[fb]).then_inc(xf_in, 16)

            def load_adj(fb, i):
                if i >= 2:
                    sp.wait_ge(mask_made, HALVES * fb + i - 1)
                    sp.wait_ge(adj_most, HALVES * fb + i - 1)
                else:
                    sp.wait_ge(mask_made, HALVES * fb)
                    sp.wait_ge(adj_most, HALVES * fb)
                c = i % 2
                sp.dma_start(adj_half[:, c, :],
                             adj_t[fb, i // 2][:, c * HALF:(c + 1) * HALF]).then_inc(adj_in[c], 16)

            def stacks(fb):
                sp.wait_ge(s_mm, TILES * fb)
                for q in range(4):
                    dst = (ks, qs)[q % 2]
                    parts = ((0, 1, 0), (0, 0, 1))[q % 2]
                    sp.wait_ge(qk_h, 4 * fb + q + 1)
                    sp.wait_ge(qk_l, 4 * fb + q + 1)
                    for h in range(HG):
                        for row, part in enumerate(parts):
                            sp.dma_start(dst[HD * row:HD * (row + 1), HG * (q // 2) + h, :].bitcast(F),
                                         stage[HD * h:HD * (h + 1), q, part, :].bitcast(F)
                                         ).then_inc(stacked[q], 16)

            def general_adj(b, general, t):
                with sp.If(general > 0):
                    sp.wait_ge(g_sel, 3 * (NT * b + t))
                    sp.dma_start(adj_gen, adj_t[b, t]).then_inc(g_adj, 16)
                with sp.If(general < 1):
                    sp.sem_inc(g_adj, 16)

            def graph(b, more):
                sp.wait_ge(y_out, 16 * NT * b)
                sp.dma_start(x1[:, :, :], x_t[b]).then_inc(x1_in, 16)
                if more:
                    load_xf(b + 1)
                    stacks(b + 1)
                    load_adj(b + 1, 0)
                    load_adj(b + 1, 1)
                sp.wait_ge(flag_made, b + 1)
                settle(sp)
                general = sp.value_load(flag[0:1, 0:1], min_val=0, max_val=1)
                sp.wait_ge(normed, QUADS * (b + 1))
                settle(sp)
                general_adj(b, general, 0)
                general_adj(b, general, 1)
                for t in range(NT):
                    if t + 2 < NT:
                        general_adj(b, general, t + 2)
                    if more and t < NT - 1:
                        load_adj(b + 1, 2 * t + 2)
                        load_adj(b + 1, 2 * t + 3)
                    if t:
                        sp.wait_ge(y_made, NT * b + t)
                        sp.dma_start(y_t[b, t - 1], x1[:, t - 1, :]).then_inc(y_out, 16)
                sp.wait_ge(y_made, NT * b + NT)
                sp.dma_start(y_t[b, NT - 1], x1[:, NT - 1, :]).then_inc(y_out, 16)

            load_xf(0)
            load_adj(0, 0)
            load_adj(0, 1)
            for i in range(2, HALVES):
                load_adj(0, i)
            sp.wait_ge(w_tr, 4)
            stacks(0)
            graph(0, True)
            with sp.Fori(1, B - 1) as b:
                graph(b, True)
            graph(B - 1, False)
            sp.wait_ge(y_out, 16 * NT * B)

        @block.gpsimd
        def _(pool):
            nc.gpsimd.memset(ident[:, :], 0.0).then_inc(consts, 1)
            pool.wait_ge(consts, 1)
            nc.gpsimd.affine_select(out=ident[:, :], in_=ident[:, :], compare_op=ALU.not_equal, fill=1.0, base=0,
                                    pattern=[[-1, P]], channel_multiplier=1).then_inc(consts, 1)
            nc.gpsimd.memset(ones[:, :], 1.0).then_inc(consts, 1)
            nc.gpsimd.memset(mhalf[:, :], -0.5).then_inc(consts, 1)
            pool.wait_ge(consts, 4)

            def masks(fb):
                for i in range(HALVES):
                    t, c = i // 2, i % 2
                    pool.wait_ge(adj_in[c], 16 * (NT * fb + t + 1))
                    pool.wait_ge(l_masked, NT * fb - NT + t + 1)
                    settle(pool)
                    nc.gpsimd.tensor_scalar(bias[:, t, c * HALF:(c + 1) * HALF], adj_half[:, c, :],
                                            0.0, BIG, ALU.is_equal, ALU.mult).then_inc(mask_made, 1)

            def front_norm(fb):
                pool.wait_ge(f_eps, fb + 1)
                settle(pool)
                nc.gpsimd.tensor_scalar(nmean[:, :], mv[:, :, 0], -1.0, None, ALU.mult).then_inc(f_rstd, 1)
                nc.gpsimd.tensor_tensor(rstd[:, :], vpe[:, :], mhalf[:, :], ALU.pow).then_inc(f_rstd, 1)
                pool.wait_ge(f_rstd, 2 * (fb + 1))
                settle(pool)
                for t in range(NT):
                    last = nc.gpsimd.tensor_scalar(xf[:, t, :], xf[:, t, :], nmean[:, t:t + 1], rstd[:, t:t + 1],
                                                   ALU.add, ALU.mult)
                last.then_inc(f_hn, 1)

            def graph(b, more):
                pool.wait_ge(x1_in, 16 * (b + 1))
                nc.gpsimd.tensor_tensor(x1[:, :, :], x1[:, :, :],
                                        bob[:, None, :].to_broadcast([P, NT, D]), ALU.add).then_inc(x1_bo, 1)
                if more:
                    front_norm(b + 1)
                pool.wait_ge(l_eps, b + 1)
                nc.gpsimd.tensor_tensor(rstd1[:, :], vpe1[:, :], mhalf[:, :], ALU.pow).then_inc(l_rstd, 1)
                if more:
                    masks(b + 1)

            front_norm(0)
            graph(0, True)
            with pool.Fori(1, B - 1) as b:
                graph(b, True)
            graph(B - 1, False)

        @block.scalar
        def _(act):
            for i, (dst, scale) in enumerate(((wqh, -SCALE), (wkh, 1.0), (wvh, 1.0))):
                act.wait_ge(w_tr, i + 1)
                nc.scalar.activation(dst[:, :, :].rearrange("p a b -> p (a b)"), (pO[0], pO[1], pT[0])[i][:, :],
                                     ACT.Copy, scale=scale).then_inc(w_h, 1)

            def front(fb, relu_h1):
                for k in range(KT):
                    act.wait_ge(f_tr, KT * fb + k + 1)
                    nc.scalar.activation(hh[:, k, :], ps[k][:, :], ACT.Relu).then_inc(f_h, 1)
                for q in range(4):
                    act.wait_ge(qk_mm, 4 * fb + q + 1)
                    act.wait_ge(av, GROUPS * fb)
                    nc.scalar.activation(stage[:, q, 0, :], ps[q % 2][:, :], ACT.Identity,
                                         bias=(bkc, bqs)[q % 2][:, q // 2:q // 2 + 1]).then_inc(qk_h, 1)
                    if q == 1:
                        relu_h1()

            def layer0(b):
                def exp(t):
                    act.wait_ge(masked, TILES * b + t + 1)
                    nc.scalar.activation(sm[:, t % RING, :], sm[:, t % RING, :], ACT.Exp, scale=-1.0,
                                         bias=mn[:, t:t + 1], accum_out=den[:, t:t + 1]).then_inc(exped, 1)

                def copy(t):
                    act.wait_ge(tr[0], TILES * b + t + 1)
                    if t >= SLOTS:
                        act.wait_ge(av, GROUPS * b + (t - SLOTS) // HG + 1)
                    else:
                        act.wait_ge(pv, NT * b)
                        act.wait_ge(stacked[t // 2], STK * (b + 1))
                    nc.scalar.copy(pt[:, t % SLOTS, 0:NT // 2, :], pT[0][:, :].rearrange("p (m n) -> p m n", n=P)
                                   ).then_inc(pt_made[0], 1)

                def rows(quad):
                    act.wait_ge(r_tr, QUADS * b + quad + 1)
                    act.wait_ge(normed, QUADS * b + quad)
                    nc.scalar.copy(rt, pO[(quad + 1) % 2][:, :]).then_inc(r_copied, 1)

                exp(0)
                for t in range(TILES):
                    if t + 1 < TILES:
                        exp(t + 1)
                    copy(t)
                    if t and t % 16 == 0:
                        rows(t // 16 - 1)
                rows(QUADS - 1)

            def layer1(b, fronts):
                for k in range(KT):
                    act.wait_ge(l_tr, KT * b + k + 1)
                    nc.scalar.copy(hh[:, k, :], ps[k][:, :]).then_inc(l_h, 1)

                def scaled(t):
                    act.wait_ge(a_sum, NT * b + t + 1)
                    if t >= 2:
                        act.wait_ge(e_ready, NT * b + t - 1)
                    for k in range(KT):
                        last = nc.scalar.activation(ah[:, t % 2, k, :], hs[:, t % 2, k, :], ACT.Copy,
                                                    scale=nacol[:, 0, k:k + 1])
                    last.then_inc(a_h, 1)

                scaled(0)
                scaled(1)
                scaled(2)

                for t in range(NT):
                    act.wait_ge(leaky, NT * b + t + 1)
                    nc.scalar.activation(sm[:, t % RING, :], sm[:, t % RING, :], ACT.Exp, scale=-1.0,
                                         bias=mnl1[:, t:t + 1], accum_out=den1[:, t:t + 1]).then_inc(l_exp, 1)
                    if t + 3 < NT:
                        scaled(t + 3)
                    act.wait_ge(ltr[0], NT * b + t + 1)
                    act.wait_ge(stacked[t // 2], STK * fronts)
                    nc.scalar.copy(pt[:, t, 0:NT // 2, :], pT[0][:, :].rearrange("p (m n) -> p m n", n=P)
                                   ).then_inc(lpt[0], 1)

            def relu_h1(b):
                for c in range(2):
                    act.wait_ge(l_hn, b + 1)
                    part = h1[:, c * NT // 2:(c + 1) * NT // 2, :]
                    nc.scalar.activation(part, part, ACT.Relu).then_inc(l_relu, 1)

            def graph(b, more):
                layer0(b)
                if more:
                    front(b + 1, lambda: relu_h1(b))
                else:
                    relu_h1(b)
                layer1(b, b + 2 if more else B)

            act.wait_ge(bqs_made, 2)
            front(0, lambda: None)
            graph(0, True)
            with act.Fori(1, B - 1) as b:
                graph(b, True)
            graph(B - 1, False)

        @block.vector
        def _(dve):
            dve.wait_ge(w_in, 16 * 12)
            nc.vector.tensor_scalar(bqs[:, :], bqc[:, :], -SCALE, None, ALU.mult).then_inc(bqs_made, 1)
            nc.vector.tensor_scalar(nacol[:, :, :], acol[:, :, :], -1.0, None, ALU.mult).then_inc(bqs_made, 1)
            dve.wait_ge(bqs_made, 2)
            for i, (dst, h, scale) in enumerate(((wql, wqh, -SCALE), (wkl, wkh, 1.0), (wvl, wvh, 1.0))):
                dve.wait_ge(w_h, i + 1)
                nc.vector.scalar_tensor_tensor(
                    out=dst[:, :, :].rearrange("p a b -> p (a b)"), in0=(pO[0], pO[1], pT[0])[i][:, :], scalar=scale,
                    in1=h[:, :, :].rearrange("p a b -> p (a b)").bitcast(F), op0=ALU.mult,
                    op1=ALU.subtract).then_inc(w_l, 1)
            dve.wait_ge(w_tr, 4)
            nc.vector.tensor_copy(wot[:, :, :].rearrange("p a b -> p (a b)"), pT[1][:, :]).then_inc(w_l, 1)

            def front_stats(fb, t):
                if t == 0:
                    dve.wait_ge(xf_in, 16 * (fb + 1))
                nc.vector.bn_stats(st[:, t, :], xf[:, t, :]).then_inc(f_stats, 1)

            def front_aggregate(fb):
                dve.wait_ge(f_stats, NT * (fb + 1))
                settle(dve)
                for t in range(NT):
                    last = nc.vector.bn_aggr(mv[:, t, :], st[:, t, :])
                last.then_inc(f_aggr, 1)
                dve.wait_ge(f_aggr, fb + 1)
                nc.vector.tensor_scalar(vpe[:, :], mv[:, :, 1], EPS, None, ALU.add).then_inc(f_eps, 1)

            def front_parts(fb):
                for k in range(KT):
                    dve.wait_ge(f_h, KT * fb + k + 1)
                    nc.vector.scalar_tensor_tensor(out=hl[:, k, :], in0=ps[k][:, :], scalar=0.0,
                                                   in1=hh[:, k, :].bitcast(F), op0=ALU.max,
                                                   op1=ALU.subtract).then_inc(f_l, 1)

            def front(fb, norm_h1):
                for q in range(4):
                    dve.wait_ge(qk_h, 4 * fb + q + 1)
                    nc.vector.scalar_tensor_tensor(
                        out=stage[:, q, 1, :], in0=ps[q % 2][:, :],
                        scalar=(bkc, bqs)[q % 2][:, q // 2:q // 2 + 1], in1=stage[:, q, 0, :].bitcast(F),
                        op0=ALU.add, op1=ALU.subtract).then_inc(qk_l, 1)
                    if q == 0:
                        norm_h1()
                    if q >= 2:
                        for t in ((0, 1), range(2, NT))[q - 2]:
                            dve.wait_ge(v_mm, NT * fb + t + 1)
                            nc.vector.tensor_tensor(v[:, t, :], (pO + pT)[t % 4][:, 0:D], bvb[:, :],
                                                    ALU.add).then_inc(v_made, 1)

            def most_half(fb, i):
                dve.wait_ge(adj_in[i % 2], 16 * (NT * fb + i // 2 + 1))
                nc.vector.tensor_reduce(most[:, i:i + 1], adj_half[:, i % 2, :], AX, ALU.max,
                                        apply_absolute_value=True).then_inc(adj_most, 1)

            def first_halves(halves):
                for i in halves:
                    most_half(0, i)
                    nc.vector.tensor_scalar(bias[:, i // 2, i % 2 * HALF:(i % 2 + 1) * HALF], adj_half[:, i % 2, :],
                                            0.0, BIG, ALU.is_equal, ALU.mult).then_inc(mask_made, 1)

            def flag_rows(fb):
                dve.wait_ge(adj_most, HALVES * (fb + 1))
                nc.vector.tensor_reduce(most_all[:, :], most[:, :], AX, ALU.max).then_inc(flag_most, 1)
                dve.wait_ge(flag_most, fb + 1)
                nc.vector.tensor_scalar(flagf[:, :], most_all[:, :], 1.5, None, ALU.is_gt).then_inc(flag_f, 1)

            def mask(b, t):
                node = t // HG % NT
                dve.wait_ge(s_mm, TILES * b + t + 1)
                dve.wait_ge(mask_made, HALVES * b + 2 * node + 2)
                if t >= RING:
                    dve.wait_ge(tr[1], TILES * b + t - RING + 1)
                else:
                    dve.wait_ge(ltr[1], NT * b)
                settle(dve)
                nc.vector.tensor_tensor_reduce(
                    out=sm[:, t % RING, :], in0=ps[t % 2][:, :], in1=bias[:, node, :], scale=1.0, scalar=3e38,
                    op0=ALU.add, op1=ALU.min, accum_out=mn[:, t:t + 1]).then_inc(masked, 1)

            def layer0(b, more):
                dve.wait_ge(flag_mm, b + 1)
                nc.vector.tensor_scalar(flag[:, :], pO[1][0:1, 0:1], 1.0, None, ALU.min).then_inc(flag_made, 1)

                def copy(t):
                    dve.wait_ge(tr[1], TILES * b + t + 1)
                    if t >= SLOTS:
                        dve.wait_ge(av, GROUPS * b + (t - SLOTS) // HG + 1)
                    else:
                        dve.wait_ge(pv, NT * b)
                        dve.wait_ge(stacked[t // 2], STK * (b + 1))
                    nc.vector.tensor_copy(pt[:, t % SLOTS, NT // 2:, :],
                                          pT[1][:, :].rearrange("p (m n) -> p m n", n=P)).then_inc(pt_made[1], 1)

                def rows(quad):
                    cols = slice(16 * quad, 16 * quad + 16)
                    dve.wait_ge(exped, TILES * b + 16 * quad + 16)
                    nc.vector.reciprocal(rden[:, cols], den[:, cols]).then_inc(r_rec, 1)
                    dve.wait_ge(r_rec, QUADS * b + quad + 1)
                    dve.wait_ge(r_tr, QUADS * b + quad)
                    nc.vector.scalar_tensor_tensor(
                        out=rb.rearrange("p (c w) -> p c w", w=HD),
                        in0=mn[:, cols].rearrange("p (c o) -> p c o", o=1).to_broadcast([P, 16, HD]), scalar=BIG / 10,
                        in1=rden[:, cols].rearrange("p (c o) -> p c o", o=1).to_broadcast([P, 16, HD]),
                        op0=ALU.is_lt, op1=ALU.mult).then_inc(r_rows, 1)

                def norm(quad):
                    dve.wait_ge(r_copied, QUADS * b + quad + 1)
                    dve.wait_ge(av, GROUPS * b + 4 * quad + 4)
                    if quad == 0:
                        dve.wait_ge(pv, NT * b)
                    nc.vector.tensor_tensor(ot[:, quad // 2, HALF * (quad % 2):HALF * (quad % 2 + 1)],
                                            pO[quad % 2][:, :], rt, ALU.mult).then_inc(normed, 1)

                for t in range(TILES):
                    if t + 2 < TILES:
                        mask(b, t + 2)
                    copy(t)
                    if t % 16 == 15:
                        rows(t // 16)
                    if t > 16 and t % 16 == 4:
                        norm(t // 16 - 1)
                    if more and 22 <= t < 22 + NT:
                        front_stats(b + 1, t - 22)
                    if more and t == 22 + NT:
                        front_aggregate(b + 1)
                norm(QUADS - 1)

            def output(b):
                dve.wait_ge(x1_bo, b + 1)
                for t in range(NT):
                    dve.wait_ge(o_mm, NT * b + t + 1)
                    nc.vector.tensor_tensor(x1[:, t, :], pT[t % 2][:, 0:D], x1[:, t, :], ALU.add).then_inc(x1_made, 1)
                    if t:
                        dve.wait_ge(x1_made, NT * b + t)
                        nc.vector.bn_stats(st1[:, t - 1, :], x1[:, t - 1, :])
                dve.wait_ge(x1_made, NT * b + NT)
                nc.vector.bn_stats(st1[:, NT - 1, :], x1[:, NT - 1, :]).then_inc(l_stats, 1)
                dve.wait_ge(l_stats, b + 1)
                settle(dve)
                for t in range(NT):
                    last = nc.vector.bn_aggr(mv1[:, t, :], st1[:, t, :])
                last.then_inc(l_aggr, 1)
                dve.wait_ge(l_aggr, b + 1)
                nc.vector.tensor_scalar(vpe1[:, :], mv1[:, :, 1], EPS, None, ALU.add).then_inc(l_eps, 1)

            def norm_h1(b):
                dve.wait_ge(l_rstd, b + 1)
                dve.wait_ge(o_mm, NT * (b + 1))
                for t in range(NT):
                    last = nc.vector.tensor_scalar(h1[:, t, :], x1[:, t, :], mv1[:, t, 0:1], rstd1[:, t:t + 1],
                                                   ALU.subtract, ALU.mult)
                last.then_inc(l_hn, 1)

            def layer1(b, fronts, more, general):
                for k in range(KT):
                    dve.wait_ge(l_h, KT * b + k + 1)
                    nc.vector.tensor_tensor(hl[:, k, :], ps[k][:, :], hh[:, k, :].bitcast(F),
                                            ALU.subtract).then_inc(l_l, 1)
                dve.wait_ge(l_l, KT * (b + 1))

                def whole(t):
                    if t >= 2:
                        dve.wait_ge(a_h, NT * b + t - 1)
                        dve.wait_ge(a_l, NT * b + t - 1)
                    cols = slice(t * P, (t + 1) * P)
                    nc.vector.tensor_tensor(hs[:, t % 2, :, :], hh[:, :, cols].bitcast(F),
                                            hl[:, :, cols].bitcast(F), ALU.add).then_inc(a_sum, 1)

                def scaled(t):
                    dve.wait_ge(a_h, NT * b + t + 1)
                    if t >= 2:
                        dve.wait_ge(e_ready, NT * b + t - 1)
                    for k in range(KT):
                        last = nc.vector.scalar_tensor_tensor(
                            out=al[:, t % 2, k, :], in0=hs[:, t % 2, k, :], scalar=nacol[:, 0, k:k + 1],
                            in1=ah[:, t % 2, k, :].bitcast(F), op0=ALU.mult, op1=ALU.subtract)
                    last.then_inc(a_l, 1)

                def select(t):
                    with dve.If(general > 0):
                        n = [GC * (NT * b + t)]

                        def link(ins):
                            n[0] = n[0] + 1
                            ins.then_inc(g_chain, 1)
                            dve.wait_ge(g_chain, n[0])
                            settle(dve)

                        dve.wait_ge(g_adj, 16 * (NT * b + t + 1))
                        dve.wait_ge(a_sum, NT * b + t + 1)
                        dve.wait_ge(g_e, 4 * (NT * b + t) + 1)
                        for k in range(1, 4):
                            for kt in range(KT):
                                last = nc.vector.tensor_scalar(hg_a[:, kt, :], hs[:, t % 2, kt, :],
                                                               nacol[:, k, kt:kt + 1], None, ALU.mult)
                                if kt < KT - 1:
                                    link(last)
                            last.then_inc(g_a, 1)
                            link(nc.vector.tensor_scalar(eq[:, :], adj_gen, float(k + 1), None, ALU.is_equal))
                            dve.wait_ge(g_e, 4 * (NT * b + t) + k + 1)
                            settle(dve)
                            link(nc.vector.copy_predicated(ps[t % 2][:, 0:HALF], eq[:, 0:HALF], pO[0][:, :]))
                            if k < 3:
                                nc.vector.copy_predicated(ps[t % 2][:, HALF:N], eq[:, HALF:N],
                                                          pO[1][:, :]).then_inc(g_sel, 1)
                                dve.wait_ge(g_sel, 3 * (NT * b + t) + k)
                            else:
                                link(nc.vector.copy_predicated(ps[t % 2][:, HALF:N], eq[:, HALF:N], pO[1][:, :]))
                        link(nc.vector.tensor_scalar(eq[:, :], adj_gen, 0.5, None, ALU.is_lt))
                        link(nc.vector.tensor_scalar(bias[:, t, :], adj_gen, 4.5, BIG, ALU.is_gt, ALU.mult))
                        nc.vector.scalar_tensor_tensor(out=bias[:, t, :], in0=eq[:, :], scalar=BIG,
                                                       in1=bias[:, t, :], op0=ALU.mult,
                                                       op1=ALU.max).then_inc(g_sel, 1)
                        dve.wait_ge(g_sel, 3 * (NT * b + t) + 3)
                        settle(dve)
                    with dve.If(general < 1):
                        dve.sem_inc(g_chain, GC)
                        dve.sem_inc(g_a, 3)
                        dve.sem_inc(g_sel, 3)

                def edge_mask(t):
                    dve.wait_ge(e_ready, NT * b + t + 1)
                    if t >= RING:
                        dve.wait_ge(ltr[1], NT * b + t - RING + 1)
                    else:
                        dve.wait_ge(tr[1], TILES * (b + 1))
                    settle(dve)
                    nc.vector.tensor_tensor_reduce(
                        out=sm[:, t % RING, :], in0=ps[t % 2][:, :], in1=bias[:, t, :], scale=1.0, scalar=3e38,
                        op0=ALU.add, op1=ALU.min, accum_out=mn1[:, t:t + 1]).then_inc(l_masked, 1)
                    dve.wait_ge(l_masked, NT * b + t + 1)
                    nc.vector.scalar_tensor_tensor(out=mnl1[:, t:t + 1], in0=mn1[:, t:t + 1], scalar=SLOPE,
                                                   in1=mn1[:, t:t + 1], op0=ALU.mult, op1=ALU.min)
                    nc.vector.scalar_tensor_tensor(out=sm[:, t % RING, :], in0=sm[:, t % RING, :], scalar=SLOPE,
                                                   in1=sm[:, t % RING, :], op0=ALU.mult,
                                                   op1=ALU.min).then_inc(leaky, 1)

                def most_tile(t):
                    most_half(b + 1, 2 * t)
                    most_half(b + 1, 2 * t + 1)

                def copy(t):
                    dve.wait_ge(ltr[1], NT * b + t + 1)
                    dve.wait_ge(stacked[t // 2], STK * fronts)
                    nc.vector.tensor_copy(pt[:, t, NT // 2:, :],
                                          pT[1][:, :].rearrange("p (m n) -> p m n", n=P)).then_inc(lpt[1], 1)

                def result(t):
                    dve.wait_ge(l_exp, NT * b + t + 1)
                    nc.vector.reciprocal(rden1[:, t:t + 1], den1[:, t:t + 1]).then_inc(l_rec, 1)
                    dve.wait_ge(l_rec, NT * b + t + 1)
                    dve.wait_ge(pv, NT * b + t + 1)
                    nc.vector.scalar_tensor_tensor(out=x1[:, t, :], in0=pO[t % 2][:, 0:D], scalar=rden1[:, t:t + 1],
                                                   in1=x1[:, t, :], op0=ALU.mult, op1=ALU.add).then_inc(y_made, 1)

                whole(0)
                whole(1)
                scaled(0)
                scaled(1)
                select(0)
                whole(2)
                edge_mask(0)
                scaled(2)
                select(1)
                for t in range(NT):
                    if t + 1 < NT:
                        edge_mask(t + 1)
                    if t + 3 < NT:
                        whole(t + 3)
                        scaled(t + 3)
                    if t + 2 < NT:
                        select(t + 2)
                    copy(t)
                    if t:
                        result(t - 1)
                    if more and t < NT - 1:
                        most_tile(t)
                if more:
                    mask(b + 1, 0)
                    mask(b + 1, 1)
                    most_tile(NT - 1)
                result(NT - 1)
                if more:
                    flag_rows(b + 1)

            def graph(b, more):
                layer0(b, more)
                if more:
                    front_parts(b + 1)
                output(b)
                if more:
                    front(b + 1, lambda: norm_h1(b))
                else:
                    norm_h1(b)
                dve.wait_ge(flag_made, b + 1)
                settle(dve)
                general = dve.value_load(flag[0:1, 0:1], min_val=0, max_val=1)
                layer1(b, b + 2 if more else B, more, general)

            for t in range(NT):
                front_stats(0, t)
            front_aggregate(0)
            first_halves(range(HALVES // 2))
            front_parts(0)
            first_halves(range(HALVES // 2, HALVES - 4))
            front(0, lambda: first_halves(range(HALVES - 4, HALVES)))
            flag_rows(0)
            mask(0, 0)
            mask(0, 1)
            graph(0, True)
            with dve.Fori(1, B - 1) as b:
                graph(b, True)
            graph(B - 1, False)

        @block.tensor
        def _(pe):
            pe.wait_ge(w_in, 16 * 12)
            pe.wait_ge(consts, 4)
            for i, out in enumerate((pO[0], pO[1], pT[0], pT[1])):
                for ft in range(KT):
                    for o in range(KT):
                        last = nc.tensor.transpose(out[:, ft * D + o * P:ft * D + (o + 1) * P],
                                                   x1[:, 2 * i + o, ft * P:(ft + 1) * P], ident[:, :])
                last.then_inc(w_tr, 1)

            def split_product(out, lhs, rhs, start, stop):
                terms = ((lhs[0], rhs[0]), (lhs[0], rhs[1]), (lhs[1], rhs[0]))
                for i, (a, c) in enumerate(terms):
                    last = nc.tensor.matmul(out, a, c, start=start and i == 0, stop=stop and i == len(terms) - 1)
                return last

            def transpose_h(src, k, done):
                for t in range(NT):
                    last = nc.tensor.transpose(ps[k][:, t * P:(t + 1) * P], src[:, t, k * P:(k + 1) * P],
                                               ident[:, :])
                last.then_inc(done, 1)

            def front_transposes(fb):
                pe.wait_ge(f_hn, fb + 1)
                pe.wait_ge(masked, TILES * fb)
                for k in range(KT):
                    transpose_h(xf, k, f_tr)

            def front(fb):
                def qk(q):
                    wh, wl = ((wkh, wkl), (wqh, wql))[q % 2]
                    pe.wait_ge(f_l, KT * (fb + 1))
                    if q >= 2:
                        pe.wait_ge(qk_l, 4 * fb + q - 1)
                    o = slice((q // 2) * P, (q // 2 + 1) * P)
                    for c in range(2):
                        n = slice(c * HALF, (c + 1) * HALF)
                        for k in range(KT):
                            last = split_product(ps[q % 2][:, n], (wh[:, k, o], wl[:, k, o]),
                                                 (hh[:, k, n], hl[:, k, n]), k == 0, k == KT - 1)
                    last.then_inc(qk_mm, 1)

                def value(t):
                    if t >= 4:
                        pe.wait_ge(v_made, NT * fb + t - 3)
                    elif t >= 2:
                        pe.wait_ge(x1_made, NT * fb)
                    else:
                        pe.wait_ge(normed, QUADS * fb)
                        pe.wait_ge(r_copied, QUADS * fb)
                    n = slice(t * P, (t + 1) * P)
                    for k in range(KT):
                        last = split_product((pO + pT)[t % 4][:, 0:D], (hh[:, k, n], hl[:, k, n]),
                                             (wvh[:, k, :], wvl[:, k, :]), k == 0, k == KT - 1)
                    last.then_inc(v_mm, 1)

                qk(0)
                qk(1)
                qk(2)
                value(0)
                value(1)
                qk(3)
                for t in range(2, NT):
                    value(t)

            def scores(b, t):
                hg, node, h = t // (HG * NT), t // HG % NT, t % HG
                head = HG * hg + h
                if t % (HG * NT) == 0:
                    pe.wait_ge(stacked[2 * hg], STK * (b + 1))
                    pe.wait_ge(stacked[2 * hg + 1], STK * (b + 1))
                if t >= 2:
                    pe.wait_ge(masked, TILES * b + t - 1)
                else:
                    pe.wait_ge(l_masked, NT * b)
                    pe.wait_ge(qk_l, 4 * (b + 1))
                for c in range(2):
                    last = nc.tensor.matmul(ps[t % 2][:, c * HALF:(c + 1) * HALF],
                                            qs[:, head, node * P:(node + 1) * P],
                                            ks[:, head, c * HALF:(c + 1) * HALF], start=True, stop=True)
                last.then_inc(s_mm, 1)

            def layer0(b):
                pe.wait_ge(y_made, NT * b)
                pe.wait_ge(v_made, NT * (b + 1))
                pe.wait_ge(flag_f, b + 1)
                nc.tensor.matmul(pO[1][0:1, 0:1], flagf[:, :], ones[:, :], start=True, stop=True).then_inc(flag_mm, 1)

                def transposes(t):
                    pe.wait_ge(exped, TILES * b + t + 1)
                    for c in range(2):
                        pe.wait_ge(pt_made[c], TILES * b + t)
                        if t == 0:
                            pe.wait_ge(lpt[c], NT * b)
                        for j in range(4):
                            m = 4 * c + j
                            last = nc.tensor.transpose(pT[c][:, j * P:(j + 1) * P],
                                                       sm[:, t % RING, m * P:(m + 1) * P], ident[:, :])
                        last.then_inc(tr[c], 1)

                def values(g, part):
                    hg, quad = g // NT, g // 4
                    if part == 0:
                        pe.wait_ge(pt_made[0], TILES * b + HG * (g + 1))
                        pe.wait_ge(pt_made[1], TILES * b + HG * (g + 1))
                    if g % 4 == 0 and quad and part == 0:
                        pe.wait_ge(r_copied, QUADS * b + quad)
                        pe.wait_ge(normed, QUADS * b + quad - 1)
                    n = slice(g % 4 * P, (g % 4 + 1) * P)
                    for m in range(NT // 4 * part, NT // 4 * (part + 1)):
                        for h in range(HG):
                            o = (HG * hg + h) * HD
                            last = nc.tensor.matmul(pO[quad % 2][HD * h:HD * (h + 1), n], v[:, m, o:o + HD],
                                                    pt[:, (HG * g + h) % SLOTS, m, :], start=(m == 0),
                                                    stop=(m == NT - 1))
                    if part == 3:
                        last.then_inc(av, 1)

                def rows(quad):
                    pe.wait_ge(r_rows, QUADS * b + quad + 1)
                    pe.wait_ge(normed, QUADS * b + quad)
                    pe.wait_ge(flag_made, b + 1)
                    for j in range(4):
                        last = nc.tensor.transpose(pO[(quad + 1) % 2][:, j * P:(j + 1) * P], rb[:, j * P:(j + 1) * P],
                                                   ident[:, :])
                    last.then_inc(r_tr, 1)

                for t in range(TILES):
                    if t + 2 < TILES:
                        scores(b, t + 2)
                    transposes(t)
                    if t >= HG:
                        values(t // HG - 1, t % HG)
                    if t and t % 16 == 0:
                        rows(t // 16 - 1)
                for part in range(4):
                    values(GROUPS - 1, part)
                rows(QUADS - 1)

            def output(b):
                pe.wait_ge(normed, QUADS * (b + 1))
                for t in range(NT):
                    if t < 2:
                        pe.wait_ge(pt_made[t], TILES * (b + 1))
                    else:
                        pe.wait_ge(x1_made, NT * b + t - 1)
                    for k in range(KT):
                        last = nc.tensor.matmul(pT[t % 2][:, 0:D], ot[:, k, t * P:(t + 1) * P], wot[:, k, :],
                                                start=(k == 0), stop=(k == KT - 1))
                    last.then_inc(o_mm, 1)

            def layer1(b, fronts, more, general):
                pe.wait_ge(l_relu, 2 * (b + 1))
                pe.wait_ge(masked, TILES * (b + 1))
                for k in range(KT):
                    pe.wait_ge(qk_l, 4 * fronts - 1 + k)
                    transpose_h(h1, k, l_tr)

                def edges(t):
                    def first():
                        pe.wait_ge(a_l, NT * b + t + 1)
                        if t >= 2:
                            pe.wait_ge(l_masked, NT * b + t - 1)
                        for c in range(2):
                            n = slice(c * HALF, (c + 1) * HALF)
                            for k in range(KT):
                                last = split_product(ps[t % 2][:, n], (ah[:, t % 2, k, :], al[:, t % 2, k, :]),
                                                     (hh[:, k, n], hl[:, k, n]), k == 0, k == KT - 1)
                        return last

                    with pe.If(general > 0):
                        first().then_inc(g_e, 1)
                        pe.wait_ge(v_made, NT * fronts)
                        pe.wait_ge(y_made, NT * b + max(t - 3, 0))
                        for kind in range(1, 4):
                            pe.wait_ge(g_a, 3 * (NT * b + t) + kind)
                            if kind > 1:
                                pe.wait_ge(g_sel, 3 * (NT * b + t) + kind - 1)
                            for c in range(2):
                                n = slice(c * HALF, (c + 1) * HALF)
                                for k in range(KT):
                                    for part in (hh, hl):
                                        last = nc.tensor.matmul(pO[c][:, :], hg_a[:, k, :],
                                                                part[:, k, n].bitcast(F),
                                                                start=(k == 0 and part is hh),
                                                                stop=(k == KT - 1 and part is hl))
                            last.then_inc(g_e, 1)
                        pe.wait_ge(g_sel, 3 * (NT * b + t) + 3)
                        pe.sem_inc(e_ready, 1)
                    with pe.If(general < 1):
                        first().then_inc(e_ready, 1)
                        pe.sem_inc(g_e, 4)

                def transposes(t):
                    pe.wait_ge(l_exp, NT * b + t + 1)
                    for c in range(2):
                        pe.wait_ge(lpt[c], NT * b + t)
                        if t == 0:
                            pe.wait_ge(x1_made, NT * (b + 1))
                            pe.wait_ge(v_made, NT * fronts)
                        for j in range(4):
                            m = 4 * c + j
                            last = nc.tensor.transpose(pT[c][:, j * P:(j + 1) * P],
                                                       sm[:, t % RING, m * P:(m + 1) * P], ident[:, :])
                        last.then_inc(ltr[c], 1)

                def values(t):
                    pe.wait_ge(lpt[0], NT * b + t + 1)
                    pe.wait_ge(lpt[1], NT * b + t + 1)
                    if t >= 2:
                        pe.wait_ge(y_made, NT * b + t - 1)
                    else:
                        pe.wait_ge(v_made, NT * fronts)
                    for m in range(NT):
                        last = nc.tensor.matmul(pO[t % 2][:, 0:D], pt[:, t, m, :], h1[:, m, :],
                                                start=(m == 0), stop=(m == NT - 1))
                    last.then_inc(pv, 1)

                edges(0)
                edges(1)
                for t in range(NT):
                    if t + 2 < NT:
                        edges(t + 2)
                    transposes(t)
                    if t:
                        values(t - 1)
                if more:
                    scores(b + 1, 0)
                    scores(b + 1, 1)
                values(NT - 1)

            def graph(b, more):
                layer0(b)
                if more:
                    front_transposes(b + 1)
                output(b)
                if more:
                    front(b + 1)
                pe.wait_ge(flag_made, b + 1)
                settle(pe)
                general = pe.value_load(flag[0:1, 0:1], min_val=0, max_val=1)
                layer1(b, b + 2 if more else B, more, general)

            pe.wait_ge(w_l, 4)
            front_transposes(0)
            front(0)
            scores(0, 0)
            scores(0, 1)
            graph(0, True)
            with pe.Fori(1, B - 1) as b:
                graph(b, True)
            graph(B - 1, False)


_INS = ["x", "adj", "L0_gnn_Wq", "L0_gnn_bq", "L0_gnn_Wk", "L0_gnn_bk", "L0_gnn_Wv", "L0_gnn_bv",
        "L0_gnn_Wo", "L0_gnn_bo", "L1_gnn_a_0", "L1_gnn_a_1", "L1_gnn_a_2", "L1_gnn_a_3"]


def kernel(**inputs):
    import numpy as _np
    import concourse.bacc as _bacc
    from concourse import mybir as _mybir
    from concourse.bass_utils import run_bass_kernel_spmd as _run

    nc = _bacc.Bacc("TRN2", target_bir_lowering=False, num_devices=1)
    arrays, args = {}, []
    for name in _INS:
        a = _np.ascontiguousarray(inputs[name])
        arrays[f"in_{name}_dram"] = a
        args.append(nc.dram_tensor(f"in_{name}_dram", a.shape, _mybir.dt.from_np(a.dtype), kind="ExternalInput").ap())
    out = nc.dram_tensor("out_0_dram", (B, N, D), F, kind="ExternalOutput").ap()
    two_graph_layers(nc, *args[:10], args[10:14], out)
    r = _run(nc, [arrays], core_ids=[0])
    return r.results[0]["out_0_dram"]
```
